# Optimizing a Trainium2 kernel written in Bass

```python
import numpy as np
import jax
import jax.numpy as jnp

def _softmax(x, axis=-1):
    return jax.nn.softmax(x, axis=axis)

def _gelu(x):
    return jax.nn.gelu(x, approximate=True)

def _silu(x):
    return jax.nn.silu(x)

def _sigmoid(x):
    return jax.nn.sigmoid(x)

def _layernorm(x, axis=-1, eps=1e-05):
    m = jnp.mean(x, axis=axis, keepdims=True)
    v = jnp.var(x, axis=axis, keepdims=True)
    return (x - m) / jnp.sqrt(v + eps)

def _scatter_add(tgt, idx, src, axis=0):
    return tgt.at[idx].add(src)

def _segment_sum(src, seg, n):
    return jax.ops.segment_sum(src, seg, n)
kernel_name = 'mk_decoder_preln_d1_seqx_r4_e0db53'

def setup_inputs(seed: int=0):
    np.random.seed(seed)
    _w = jnp.asarray

    def _rec_inputs():
        import jax
        import jax.numpy as jnp
        _rk = jax.random.key(seed)
        x = 7.22e-05 + 1 * jax.random.normal(jax.random.fold_in(_rk, 1), (64, 128, 512), jnp.float32)
        _lenS = 128 - jax.random.randint(jax.random.fold_in(_rk, 7), (64,), 0, max(1, 128 // 4) + 1, jnp.int32)
        _lenS2 = 128 - jax.random.randint(jax.random.fold_in(_rk, 8), (64,), 0, max(1, 128 // 4) + 1, jnp.int32)
        _ctx_2048P = jax.random.normal(jax.random.fold_in(_rk, 11), (64, 16, 512), jnp.float32)
        _ctx_2048c = jax.random.dirichlet(jax.random.fold_in(_rk, 511), 0.3 * jnp.ones((16,), jnp.float32), (64, 128))
        _ctx_2048t = jnp.einsum('bsk,bkd->bsd', _ctx_2048c, _ctx_2048P)
        _ctx_2048t = _ctx_2048t * jax.lax.rsqrt(jnp.mean(jnp.square(_ctx_2048t)) + 1e-12) * 0.953939
        ctx_2048 = 4.13588e-05 + 0.999923 * (_ctx_2048t + 0.3 * jax.random.normal(jax.random.fold_in(_rk, 611), (64, 128, 512), jnp.float32))
        return (x, ctx_2048)
    x, ctx_2048 = _rec_inputs()

    def _L0_attn_setup():
        import jax, jax.numpy as jnp
        import numpy as np
        B, L, H, I, N, R, K = (2, 256, 512, 1024, 16, 128, 4)
        key = jax.random.key(seed)
        ks = jax.random.split(key, 8)
        sc = lambda k, shape, s: jax.random.normal(k, shape, dtype=jnp.float32) * s
        x = jax.random.normal(ks[0], (B, L, H), dtype=jnp.float32)
        in_proj_w = sc(ks[1], (2 * I, H), 0.02)
        conv_w = sc(ks[2], (I, 1, K), 0.2)
        conv_b = jnp.zeros((I,), jnp.float32)
        x_proj_w = sc(ks[3], (R + 2 * N, I), 0.02)
        dt_proj_w = sc(ks[4], (I, R), 0.05)
        dt_proj_b = sc(ks[5], (I,), 0.5) - 2.0
        A_log = jnp.log(jnp.broadcast_to(jnp.arange(1, N + 1, dtype=jnp.float32)[None, :], (I, N)))
        D = jnp.ones((I,), jnp.float32)
        out_proj_w = sc(ks[6], (H, I), 0.02)
        return dict(x=x, in_proj_w=in_proj_w, conv_w=conv_w, conv_b=conv_b, x_proj_w=x_proj_w, dt_proj_w=dt_proj_w, dt_proj_b=dt_proj_b, A_log=A_log, D=D, out_proj_w=out_proj_w)
    _L0_attn_all = _L0_attn_setup()
    _L0_attn_in = {k: v for k, v in _L0_attn_all.items() if k in ('in_proj_w', 'conv_w', 'conv_b', 'x_proj_w', 'dt_proj_w', 'dt_proj_b', 'A_log', 'D', 'out_proj_w')}
    del _L0_attn_all

    def _L0_xattn_setup():
        import jax, jax.numpy as jnp
        import numpy as np
        N, E, T, H = (8, 128, 512, 8)
        key = jax.random.key(seed)
        ks = jax.random.split(key, 6)
        s = 1.0 / np.sqrt(E)
        return {'mask': jax.random.normal(ks[0], (N, E, T), jnp.float32), 'encodings': jax.random.normal(ks[1], (N, E, T), jnp.float32), 'w_in': jax.random.normal(ks[2], (3 * E, E), jnp.float32) * s, 'b_in': jnp.zeros((3 * E,), jnp.float32), 'w_out': jax.random.normal(ks[3], (E, E), jnp.float32) * s, 'b_out': jnp.zeros((E,), jnp.float32), 'w_ct': jax.random.normal(ks[4], (E, E), jnp.float32) * s, 'b_ct': jnp.zeros((E,), jnp.float32), 'local_size': 64}
    _L0_xattn_all = _L0_xattn_setup()
    _L0_xattn_in = {k: v for k, v in _L0_xattn_all.items() if k in ('w_in', 'b_in', 'w_out', 'b_out', 'w_ct', 'b_ct')}
    del _L0_xattn_all

    def _L0_ffn_setup():
        import jax, jax.numpy as jnp
        import numpy as np
        H = 512
        E = 8
        K = 2
        I = 16
        key = jax.random.key(seed)
        k1, k2, k3, k4 = jax.random.split(key, 4)
        B, T = (2, 1024)
        x = jax.random.normal(k1, (B, T, H), dtype=jnp.float32)
        router_w = jax.random.normal(k2, (E, H), dtype=jnp.float32) / np.sqrt(H)
        down_w = jax.random.normal(k3, (E, I, H), dtype=jnp.float32) / np.sqrt(H)
        up_w = jax.random.normal(k4, (E, H, I), dtype=jnp.float32) / np.sqrt(I)
        return {'x': x, 'router_w': router_w, 'down_w': down_w, 'up_w': up_w}
    _L0_ffn_all = _L0_ffn_setup()
    _L0_ffn_in = {k: v for k, v in _L0_ffn_all.items() if k in ('router_w', 'down_w', 'up_w')}
    del _L0_ffn_all
    return {'x': x, 'ctx_2048': ctx_2048, 'L0_attn_in_proj_w': _L0_attn_in['in_proj_w'], 'L0_attn_conv_w': _L0_attn_in['conv_w'], 'L0_attn_conv_b': _L0_attn_in['conv_b'], 'L0_attn_x_proj_w': _L0_attn_in['x_proj_w'], 'L0_attn_dt_proj_w': _L0_attn_in['dt_proj_w'], 'L0_attn_dt_proj_b': _L0_attn_in['dt_proj_b'], 'L0_attn_A_log': _L0_attn_in['A_log'], 'L0_attn_D': _L0_attn_in['D'], 'L0_attn_out_proj_w': _L0_attn_in['out_proj_w'], 'L0_xattn_w_in': _L0_xattn_in['w_in'], 'L0_xattn_b_in': _L0_xattn_in['b_in'], 'L0_xattn_w_out': _L0_xattn_in['w_out'], 'L0_xattn_b_out': _L0_xattn_in['b_out'], 'L0_xattn_w_ct': _L0_xattn_in['w_ct'], 'L0_xattn_b_ct': _L0_xattn_in['b_ct'], 'L0_ffn_router_w': _L0_ffn_in['router_w'], 'L0_ffn_down_w': _L0_ffn_in['down_w'], 'L0_ffn_up_w': _L0_ffn_in['up_w']}

def reference(x, ctx_2048, L0_attn_in_proj_w, L0_attn_conv_w, L0_attn_conv_b, L0_attn_x_proj_w, L0_attn_dt_proj_w, L0_attn_dt_proj_b, L0_attn_A_log, L0_attn_D, L0_attn_out_proj_w, L0_xattn_w_in, L0_xattn_b_in, L0_xattn_w_out, L0_xattn_b_out, L0_xattn_w_ct, L0_xattn_b_ct, L0_ffn_router_w, L0_ffn_down_w, L0_ffn_up_w):
    import jax
    import jax.numpy as jnp

    def _L0_attn_ref(x, in_proj_w, conv_w, conv_b, x_proj_w, dt_proj_w, dt_proj_b, A_log, D, out_proj_w):
        import jax, jax.numpy as jnp
        import numpy as np
        B, L, H, I, N, R, K = (2, 256, 512, 1024, 16, 128, 4)
        nI, nK = (conv_w.shape[0], conv_w.shape[2])
        nR = dt_proj_w.shape[1]
        nN = A_log.shape[1]
        proj = jnp.einsum('blh,ph->blp', x, in_proj_w)
        h_in, gate = jnp.split(proj, 2, axis=-1)
        hc = jnp.transpose(h_in, (0, 2, 1))
        hc = jax.lax.conv_general_dilated(hc, conv_w, (1,), [(nK - 1, 0)], dimension_numbers=('NCH', 'OIH', 'NCH'), feature_group_count=nI)
        u = jax.nn.silu(hc + conv_b[None, :, None])
        uT = jnp.transpose(u, (0, 2, 1))
        ssm = jnp.einsum('bli,pi->blp', uT, x_proj_w)
        ts, Bm, Cm = jnp.split(ssm, [nR, nR + nN], axis=-1)
        dt = jax.nn.softplus(jnp.einsum('blr,ir->bli', ts, dt_proj_w) + dt_proj_b)
        A = -jnp.exp(A_log)
        dA = jnp.exp(dt[..., None] * A[None, None])
        dBx = (dt * uT)[..., None] * Bm[:, :, None, :]

        def combine(c1, c2):
            a1, b1 = c1
            a2, b2 = c2
            return (a2 * a1, a2 * b1 + b2)
        _, hstates = jax.lax.associative_scan(combine, (dA, dBx), axis=1)
        y = jnp.einsum('blin,bln->bli', hstates, Cm) + D * uT
        y = y * jax.nn.silu(gate)
        return jnp.einsum('bli,hi->blh', y, out_proj_w)

    def _L0_xattn_ref(mask, encodings, w_in, b_in, w_out, b_out, w_ct, b_ct, local_size):
        import jax, jax.numpy as jnp
        import numpy as np
        N, E, T, H = (8, 128, 512, 8)
        n, e, t = mask.shape
        d = e // H
        x = jnp.transpose(mask, (0, 2, 1))
        qkv = x @ w_in.T + b_in
        q, k, v = jnp.split(qkv, 3, axis=-1)
        q = q.reshape(n, t, H, d)
        k = k.reshape(n, t, H, d)
        v = v.reshape(n, t, H, d)
        scores = jnp.einsum('bqhd,bkhd->bhqk', q, k) / jnp.sqrt(jnp.asarray(d, q.dtype))
        idx = jnp.arange(t)
        band = jnp.abs(idx[:, None] - idx[None, :]) <= local_size
        neg = jnp.asarray(jnp.finfo(scores.dtype).min, scores.dtype)
        scores = jnp.where(band[None, None], scores, neg)
        attn = jax.nn.softmax(scores, axis=-1)
        o = jnp.einsum('bhqk,bkhd->bqhd', attn, v).reshape(n, t, e)
        o = o @ w_out.T + b_out
        o = jnp.transpose(o, (0, 2, 1))
        y = jax.nn.relu(o) * encodings
        out = jnp.einsum('nit,io->not', y, w_ct) + b_ct[None, :, None]
        return out

    def _L0_ffn_ref(x, router_w, down_w, up_w):
        import jax, jax.numpy as jnp
        import numpy as np
        H = 512
        E = 8
        K = 2
        I = 16
        logits = jnp.einsum('bth,eh->bte', x, router_w)
        weights = jax.nn.softmax(logits, axis=-1)
        top_w, top_idx = jax.lax.top_k(weights, K)
        topk_mask = jnp.sum(jax.nn.one_hot(top_idx, E, dtype=x.dtype), axis=-2)
        gate = weights * topk_mask
        h = jnp.einsum('bth,eih->beti', x, down_w)
        a = jax.nn.silu(h)
        expert_out = jnp.einsum('beti,ehi->beth', a, up_w)
        out = jnp.einsum('beth,bte->bth', expert_out, gate)
        return out
    x = x + _L0_attn_ref(_layernorm(x, axis=-1), L0_attn_in_proj_w, L0_attn_conv_w, L0_attn_conv_b, L0_attn_x_proj_w, L0_attn_dt_proj_w, L0_attn_dt_proj_b, L0_attn_A_log, L0_attn_D, L0_attn_out_proj_w)
    x = x + _L0_xattn_ref(_layernorm(x, axis=-1), ctx_2048, L0_xattn_w_in, L0_xattn_b_in, L0_xattn_w_out, L0_xattn_b_out, L0_xattn_w_ct, L0_xattn_b_ct, 64)
    x = x + _L0_ffn_ref(_layernorm(x, axis=-1), L0_ffn_router_w, L0_ffn_down_w, L0_ffn_up_w)
    return x

_drawn_inputs = setup_inputs


def setup_inputs(seed=0):
    import zlib

    import numpy as np

    out = dict(_drawn_inputs(seed))
    spreads = {'L0_attn_conv_b': (0.0, 0.497),
     'L0_attn_D': (1.0, 0.6),
     'L0_xattn_b_in': (0.0, 0.1),
     'L0_xattn_b_out': (0.0, 0.1),
     'L0_xattn_b_ct': (0.0, 0.1)}
    factors = {'L0_attn_x_proj_w': 8.0,
     'L0_attn_dt_proj_w': 8.0,
     'L0_attn_dt_proj_b': 8.0,
     'L0_attn_A_log': 8.0}
    for name, (base, spread) in spreads.items():
        noise = np.random.default_rng([zlib.crc32(name.encode()), seed]).standard_normal(out[name].shape)
        drawn = base * np.exp(spread * noise) if base else spread * noise
        out[name] = jnp.asarray(drawn.astype(out[name].dtype))
    for name, factor in factors.items():
        out[name] = (out[name] * factor).astype(out[name].dtype)
    return out
```

```python
import concourse.bass as bass
from concourse import mybir
from contextlib import ExitStack


def decoder_layer(nc, x_d, ctx_d, w_in_d, conv_w_d, conv_b_d, w_xt_d, w_xbc_d, w_dt_d, dt_b_d, a_log_d,
                  d_skip_d, w_outp_d, w_qk_d, b_qk_d, w_v_d, b_v_d, w_o_d, b_o_d, w_ct_d, b_ct_d,
                  w_router_d, w_down_d, w_up_d, ident_d, ident_bf_d, band_d, stack_d, den_d, iota_d, out_d):
    F32, BF, U32 = mybir.dt.float32, mybir.dt.bfloat16, mybir.dt.uint32
    ALU, ACT, AX = mybir.AluOpType, mybir.ActivationFunctionType, mybir.AxisListType

    P = 128
    B, T, H = x_d.shape
    GB = 4
    NG = B // GB
    NT = GB * T
    KH = H // P
    I = w_outp_d.shape[1] * P
    NI = I // P
    N = a_log_d.shape[2]
    KC = conv_w_d.shape[2]
    NHEAD, DH = 8, 16
    NJ = 2
    NE = w_router_d.shape[2]
    EPS = 1e-5
    NB4 = H // P
    WIN = 2 * P
    RING = 8
    DAR = 4
    POOL_C = (1, 4, 7, 10, 12)
    NPC = len(POOL_C)
    NDC = N - NPC
    LAG = 3

    stack = ExitStack()
    with stack:
        def sb(name, shape, dt=F32):
            return stack.enter_context(nc.sbuf_tensor(name, shape, dt))

        def sem(name):
            return stack.enter_context(nc.semaphore(name))

        w_in = sb("w_in", [P, KH, 2 * I])
        conv_w = sb("conv_w", [P, NI, KC])
        conv_b = sb("conv_b", [P, NI])
        w_xt = sb("w_xt", [P, NI, P])
        w_xbc = sb("w_xbc", [P, NI, 96])
        dt_b = sb("dt_b", [P, NI])
        a_neg = sb("a_neg", [P, NI, N])
        d_skip = sb("d_skip", [P, NI])
        w_outp = sb("w_outp", [P, NI, H])
        w_qk = sb("w_qk", [P, 4, P])
        b_qk = sb("b_qk", [P, 4])
        w_v = sb("w_v", [P, P])
        b_v = sb("b_v", [P, NJ])
        w_o = sb("w_o", [P, NJ, P])
        b_o = sb("b_o", [P, 1])
        w_ct = sb("w_ct", [P, P])
        b_ct = sb("b_ct", [P, 1])
        w_router = sb("w_router", [P, KH, NE])
        w_down = sb("w_down", [P, KH, P])
        w_up = sb("w_up", [P, H])
        ident = sb("ident", [P, P])
        ident_bf = sb("ident_bf", [P, P], BF)
        band = sb("band", [P, 2, WIN], BF)
        stack3 = sb("stack3", [96, 32], BF)
        den_sel = sb("den_sel", [P, P])
        iota = sb("iota", [P, NE])
        neg_half = sb("neg_half", [P, GB])
        held = sb("held", [P, 1])
        x = sb("x", [P, GB, H])
        u = sb("u", [P, NI, NT])
        gate = sb("gate", [P, NI, NT])
        ring = sb("ring", [P, RING, NT])
        delta = sb("delta", [P, 2, NT])
        du = sb("du", [P, 2, NT])
        soft = sb("soft", [P, NT])
        tmp = sb("tmp", [P, NT])
        y_tmp = sb("y_tmp", [P, NT])
        ts = sb("ts", [P, NT])
        w_dt = sb("w_dt", [P, 2, P])
        ln_st = sb("ln_st", [P, GB, 6])
        ln_mv = sb("ln_mv", [P, GB, 2])
        ln_rs = sb("ln_rs", [P, GB])
        shared = sb("shared", [P, 32 * NT])

        def part(at, *dims):
            size = 1
            for d in dims:
                size *= d
            v = shared[:, at:at + size]
            if len(dims) == 1:
                return v
            names = "abcd"[:len(dims)]
            return v.rearrange("p (" + " ".join(names) + ") -> p " + " ".join(names),
                               **dict(zip(names, dims)))

        bc = part(0, 2 * N, NT)
        xn = part(0, GB, H)
        xt = part(2048, KH, NT)
        hc0 = part(4096, 2, NT)
        probs = part(0, NB4, 2, 4, WIN)
        qk = part(8192, 4, H)
        o_sb = part(10240, NJ, H)
        rden = part(11264, NJ, H)
        relu_o = part(12288, H)
        xb = part(12800, H)
        enc = part(13312, H)
        v_aug = part(13824, NB4, NHEAD, 32)
        nmax = part(14848, NB4, NJ, P)
        act_e = part(4096, NT)
        gated = part(4608, NT)
        g_rep = part(5120, GB, NE, 16)
        small = part(6000, 16 * 32)
        bc_hi = ring[0:96, 0, 0:NT // 2].bitcast(BF)
        bc_mid = ring[0:96, 1, 0:NT // 2].bitcast(BF)
        bc_r1 = ring[0:96, 2, :]
        bc_r2 = ring[0:96, 3, :]
        bc_st = ring[0:96, 4, 0:NT // 2].bitcast(BF)

        ps = stack.enter_context(nc.psum_tensor("ps", [P, 8, 512], F32))

        w_loaded = sem("w_loaded")
        x_in, x_out, enc_in = sem("x_in"), sem("x_out"), sem("enc_in")
        dtw_in = [sem("dtw_in_even"), sem("dtw_in_odd")]
        const_done, setup_done, a_exp = sem("const_done"), sem("setup_done"), sem("a_exp")
        bo_ps, bo_done = sem("bo_ps"), sem("bo_done")
        ln_stat, ln_aggr, ln_eps, ln_rstd, ln_out = (sem("ln_stat"), sem("ln_aggr"), sem("ln_eps"),
                                                     sem("ln_rstd"), sem("ln_out"))
        xt_ps, xt_done = sem("xt_ps"), sem("xt_done")
        hin_ps, gin_ps, tap3_done, tap_done, conv_done, u_done, gate_done = (
            sem("hin_ps"), sem("gin_ps"), sem("tap3_done"), sem("tap_done"), sem("conv_done"),
            sem("u_done"), sem("gate_done"))
        ts_ps, ts_done, bc_ps, split_done = sem("ts_ps"), sem("ts_done"), sem("bc_ps"), sem("split_done")
        rep_ps, rep_a, rep_v = sem("rep_ps"), sem("rep_a"), sem("rep_v")
        da_zeroed = sem("da_zeroed")
        dt_ps, sp_abs, sp_exp, sp_ln, sp_r, sp_c, sp_d, relu_dt, dt_done, du_done = (
            sem("dt_ps"), sem("sp_abs"), sem("sp_exp"), sem("sp_ln"), sem("sp_r"), sem("sp_c"),
            sem("sp_d"), sem("relu_dt"), sem("dt_done"), sem("du_done"))
        da_done, dbx_done, h_done, hcd_done, hcp_done, hc_used = (
            sem("da_done"), sem("dbx_done"), sem("h_done"), sem("hcd_done"), sem("hcp_done"), sem("hc_used"))
        y_sum, y_done, outp_ps, x1_done = sem("y_sum"), sem("y_done"), sem("outp_ps"), sem("x1_done")
        att_zero = sem("att_zero")
        xb_done, qk_ps, qk_done, v_ps, v_done = (sem("xb_done"), sem("qk_ps"), sem("qk_done"),
                                                 sem("v_ps"), sem("v_done"))
        s_ps, max_done, shift_ps, q_done = sem("s_ps"), sem("max_done"), sem("shift_ps"), sem("q_done")
        st_ps, p_done, o_ps, o_done = sem("st_ps"), sem("p_done"), sem("o_ps"), sem("o_done")
        den_ps, rden_done, on_done, wo_ps = sem("den_ps"), sem("rden_done"), sem("on_done"), sem("wo_ps")
        relu_done, enc_used, ct_ps, x2_done = (sem("relu_done"), sem("enc_used"), sem("ct_ps"),
                                               sem("x2_done"))
        down_ps, act_done, logit_ps, small_done, lexp_done, grep_done, gt_ps, gated_done = (
            sem("down_ps"), sem("act_done"), sem("logit_ps"), sem("small_done"), sem("lexp_done"),
            sem("grep_done"), sem("gt_ps"), sem("gated_done"))
        gate_step, up_ps, x3_done = sem("gate_step"), sem("up_ps"), sem("x3_done")

        H0 = DAR
        U0 = RING
        NSMALL = 13

        resident = [(w_in, w_in_d), (conv_w, conv_w_d), (conv_b, conv_b_d), (w_xt, w_xt_d),
                    (w_xbc, w_xbc_d), (dt_b, dt_b_d), (a_neg, a_log_d), (d_skip, d_skip_d),
                    (w_outp, w_outp_d), (w_qk, w_qk_d), (b_qk, b_qk_d), (w_v, w_v_d), (b_v, b_v_d),
                    (w_o, w_o_d), (b_o, b_o_d), (w_ct, w_ct_d), (b_ct, b_ct_d), (w_router, w_router_d),
                    (w_down, w_down_d), (w_up, w_up_d), (ident, ident_d), (ident_bf, ident_bf_d),
                    (band, band_d), (stack3, stack_d), (den_sel, den_d), (iota, iota_d)]
        ALL_W = 16 * len(resident)

        def window(blk):
            lo = 64 if blk == 0 else 0
            hi = WIN - 64 if blk == NB4 - 1 else WIN
            return lo, hi, blk * P - 64 + lo

        block = stack.enter_context(nc.Block())

        @block.sync
        def _(sp):
            for dst, src in resident:
                sp.dma_start(dst[:], src).then_inc(w_loaded, 16)
            with sp.Fori(0, NG) as g:
                sp.wait_ge(x_out, g * 16 + 1)
                sp.dma_start(x[:], x_d[bass.ds(g * GB, GB)].rearrange("b t h -> t b h")).then_inc(x_in, 16)
                with sp.Fori(0, NI // 2) as m:
                    for p in range(2):
                        c = g * NI + m * 2 + p
                        sp.wait_ge(dt_ps, c + 1)
                        sp.dma_start(w_dt[:, p, :], w_dt_d[:, bass.ds((m * 2 + p) * P, P)]).then_inc(dtw_in[p], 16)
                with sp.Fori(0, GB) as b:
                    sp.wait_ge(enc_used, g * GB + b + 1)
                    sp.wait_ge(x1_done, (g + 1) * GB)
                    sp.dma_start(enc, ctx_d[g * GB + b]).then_inc(enc_in, 16)
                sp.wait_ge(x3_done, (g + 1) * GB)
                sp.dma_start(out_d[bass.ds(g * GB, GB)].rearrange("b t h -> t b h"), x[:]).then_inc(x_out, 16)
            sp.wait_ge(x_out, NG * 16 + 1)

        @block.gpsimd
        def _(pool):
            nc.gpsimd.memset(neg_half[:], -0.5).then_inc(const_done, 1)
            pool.wait_ge(const_done, 1)

            def rstd(use, g):
                pool.wait_ge(ln_eps, g * 3 + use + 1)
                nc.gpsimd.tensor_tensor(ln_rs[:], ln_rs[:], neg_half[:], ALU.pow).then_inc(ln_rstd, 1)

            def times_c(k, p, n, slot):
                pool.wait_ge(h_done, H0 + 1 + k)
                nc.gpsimd.tensor_tensor(ring[:, slot, :], ring[:, slot, :], bc[:, N + n, :],
                                        ALU.mult).then_inc(hcp_done, 1)

            with pool.Fori(0, NG) as g:
                rstd(0, g)
                with pool.Fori(0, NI // 2) as m:
                    for p in range(2):
                        c = g * NI + m * 2 + p
                        if p == 0:
                            pool.wait_ge(rep_a, (g + 1) * 4)
                            pool.wait_ge(rep_v, (g + 1) * 4)
                        pool.wait_ge(du_done, c + 2)
                        for n in range(N):
                            pool.wait_ge(hc_used, c * N + n + 1)
                            nc.gpsimd.tensor_tensor(ring[:, n % RING, :], du[:, p, :], bc[:, n, :],
                                                    ALU.mult).then_inc(dbx_done, 1)
                            if n - LAG in POOL_C:
                                times_c(c * N + n - LAG, p, n - LAG, (n - LAG) % RING)
                rstd(1, g)
                nc.gpsimd.memset(v_aug[:, :, :, DH + 1:32], 0.0).then_inc(att_zero, 1)
                nc.gpsimd.memset(nmax, 0.0).then_inc(att_zero, 1)
                nc.gpsimd.memset(v_aug[:, :, :, DH:DH + 1], 1.0).then_inc(att_zero, 1)
                rstd(2, g)

        @block.scalar
        def _(act):
            act.wait_ge(w_loaded, ALL_W)
            nc.scalar.activation(a_neg[:], a_neg[:], ACT.Exp).then_inc(a_exp, 1)
            act.wait_ge(bo_ps, 1)
            nc.scalar.activation(b_o[:], ps[:, 0, 0:1], ACT.Identity, bias=b_o[:]).then_inc(bo_done, 1)
            act.wait_ge(bo_done, 1)
            act.wait_ge(setup_done, 2)

            def transposed(g, use):
                for k in range(KH):
                    act.wait_ge(xt_ps, g * 2 * KH + use * KH + k + 1)
                    nc.scalar.copy(xt[:, k, :], ps[:, k, :]).then_inc(xt_done, 1)

            def soft_parts(c, ic, p):
                act.wait_ge(dt_ps, c + 3)
                act.wait_ge(du_done, c + 1)
                nc.scalar.activation(soft[:], ps[:, 6 + p, :], ACT.Abs, bias=dt_b[:, bass.ds(ic, 1)]).then_inc(sp_abs, 1)
                act.wait_ge(sp_abs, c + 1)
                nc.scalar.activation(soft[:], soft[:], ACT.Exp, scale=-1.0).then_inc(sp_exp, 1)
                act.wait_ge(sp_exp, c + 1)
                nc.scalar.activation(delta[:, p, :], soft[:], ACT.Ln, bias=1.0).then_inc(sp_ln, 1)

            def decays(c, ic, p, ahead):
                act.wait_ge(dt_done, c + 2)
                d_in = delta[:, p, :].rearrange("p (b t) -> p b t", b=GB)[:, :, 1:T]
                for n in range(N):
                    act.wait_ge(h_done, c * N + n + 1)
                    nc.scalar.activation(
                        ps[:, n % DAR, :].rearrange("p (b t) -> p b t", b=GB)[:, :, 1:T], d_in, ACT.Exp,
                        scale=a_neg[:, bass.ds(ic, 1), n]).then_inc(da_done, 1)
                    if n == 4 and ahead:
                        soft_parts(c + 1, ic + 1, 1 - p)

            def exps(blk, pair, st, i):
                lo, hi, _ = window(blk)
                bank = 2 * (st % 3)
                act.wait_ge(st_ps, i * 8 + st + 1)
                nc.scalar.activation(
                    probs[:, blk, :, 2 * pair:2 * pair + 2, lo:hi].rearrange("p j a w -> p a j w"),
                    ps[:, bank:bank + 2, :].rearrange("p a (j w) -> p a j w", j=NJ)[:, :, :, lo:hi],
                    ACT.Exp).then_inc(p_done, 1)

            with act.Fori(0, NG) as g:
                transposed(g, 0)
                for ic in range(NI):
                    if ic >= 2:
                        act.wait_ge(u_done, g * NI + ic - 1)
                    act.wait_ge(hin_ps, g * NI + ic + 1)
                    nc.scalar.activation(hc0[:, ic % 2, :], ps[:, 4 + ic % 2, :], ACT.Identity,
                                         scale=conv_w[:, ic, KC - 1:KC], bias=conv_b[:, ic:ic + 1]).then_inc(tap3_done, 1)
                    act.wait_ge(gin_ps, g * NI + ic + 1)
                    nc.scalar.activation(gate[:, ic, :], ps[:, 6 + ic % 2, :], ACT.Silu).then_inc(gate_done, 1)
                    if ic:
                        act.wait_ge(conv_done, g * NI + ic)
                        nc.scalar.activation(u[:, ic - 1, :], hc0[:, (ic - 1) % 2, :], ACT.Silu).then_inc(u_done, 1)
                act.wait_ge(conv_done, (g + 1) * NI)
                nc.scalar.activation(u[:, NI - 1, :], hc0[:, (NI - 1) % 2, :], ACT.Silu).then_inc(u_done, 1)
                act.wait_ge(ts_ps, g + 1)
                nc.scalar.copy(ts[:], ps[:, 0, :]).then_inc(ts_done, 1)
                for q in range(0, 8, 2):
                    act.wait_ge(rep_ps, g * 8 + q + 1)
                    nc.scalar.copy(bc[:, 4 * q:4 * q + 4, :], ps[:, 0:4, :]).then_inc(rep_a, 1)
                soft_parts(g * NI, 0, 0)
                act.wait_ge(da_zeroed, g + 1)
                with act.Fori(0, NI // 2 - 1) as m:
                    decays(g * NI + m * 2, m * 2, 0, True)
                    decays(g * NI + m * 2 + 1, m * 2 + 1, 1, True)
                decays(g * NI + NI - 2, NI - 2, 0, True)
                decays(g * NI + NI - 1, NI - 1, 1, False)
                with act.Fori(0, GB) as b:
                    i = g * GB + b
                    for j in range(4):
                        act.wait_ge(qk_ps, i * 4 + j + 1)
                        nc.scalar.activation(qk[:, j, :], ps[:, j, :], ACT.Identity, scale=0.25 if j < 2 else 1.0,
                                             bias=b_qk[:, j:j + 1]).then_inc(qk_done, 1)
                    for st in range(8):
                        exps(st // 2, st % 2, st, i)
                    for j in range(NJ):
                        act.wait_ge(o_ps, i + 1)
                        nc.scalar.copy(o_sb[:, j, :], ps[:, 6 + j, :]).then_inc(o_done, 1)
                    act.wait_ge(wo_ps, i + 1)
                    nc.scalar.activation(relu_o, ps[:, 2, :], ACT.Relu, bias=b_o[:]).then_inc(relu_done, 1)
                transposed(g, 1)
                act.wait_ge(down_ps, g + 1)
                nc.scalar.activation(act_e, ps[:, 4, :], ACT.Silu).then_inc(act_done, 1)
                act.wait_ge(small_done, g * NSMALL + 6)
                nc.scalar.activation(small[:, 64:96], small[:, 64:96], ACT.Exp).then_inc(lexp_done, 1)

        @block.tensor
        def _(pe):
            pe.wait_ge(w_loaded, ALL_W)
            nc.tensor.matmul(ps[:, 0, 0:1], w_o[:, 0, :], b_v[:, 0:1], start=True, stop=False)
            nc.tensor.matmul(ps[:, 0, 0:1], w_o[:, 1, :], b_v[:, 1:2], start=False, stop=True).then_inc(bo_ps, 1)
            pe.wait_ge(bo_done, 1)

            def transposes(g, use):
                pe.wait_ge(ln_out, g * 2 * GB + use * GB + GB)
                for k in range(KH):
                    for b in range(GB):
                        last = nc.tensor.transpose(ps[:, k, b * T:(b + 1) * T], xn[:, b, k * P:(k + 1) * P], ident[:])
                    last.then_inc(xt_ps, 1)

            def dt_product(c, pr, p):
                pe.wait_ge(dtw_in[p], (pr + 1) * 16)
                pe.wait_ge(relu_dt, c + 1)
                nc.tensor.matmul(ps[:, 6 + p, :], w_dt[:, p, :], ts[:], start=True, stop=True).then_inc(dt_ps, 1)

            def sums(c, pr, p, ahead):
                for n in range(N):
                    if n in POOL_C:
                        pe.wait_ge(hcp_done, c * NPC + POOL_C.index(n) + 1)
                    else:
                        pe.wait_ge(hcd_done, c * NDC + len([a for a in range(n) if a not in POOL_C]) + 1)
                    nc.tensor.matmul(ps[:, 4 + p, :], ident[:], ring[:, n % RING, :],
                                     start=(n == 0), stop=(n == N - 1)).then_inc(hc_used, 1)
                    if n == 0 and ahead:
                        dt_product(c + 1, pr + p, 1 - p)

            with pe.Fori(0, NG) as g:
                transposes(g, 0)
                for ic in range(NI):
                    for half, bank, made in ((0, 4, hin_ps), (1, 6, gin_ps)):
                        if ic >= 2:
                            pe.wait_ge((conv_done, gate_done)[half], g * NI + ic - 1)
                        for k in range(KH):
                            if ic == 0:
                                pe.wait_ge(xt_done, g * 2 * KH + k + 1)
                            col = half * I + ic * P
                            last = nc.tensor.matmul(ps[:, bank + ic % 2, :], w_in[:, k, col:col + P], xt[:, k, :],
                                                    start=(k == 0), stop=(k == KH - 1))
                        last.then_inc(made, 1)
                for ic in range(NI):
                    pe.wait_ge(u_done, g * NI + ic + 1)
                    t_last = nc.tensor.matmul(ps[:, 0, :], w_xt[:, ic, :], u[:, ic, :],
                                              start=(ic == 0), stop=(ic == NI - 1))
                    b_last = nc.tensor.matmul(ps[0:96, 1, :], w_xbc[:, ic, :], u[:, ic, :],
                                              start=(ic == 0), stop=(ic == NI - 1))
                t_last.then_inc(ts_ps, 1)
                b_last.then_inc(bc_ps, 1)
                pe.wait_ge(split_done, g * 6 + 6)
                pe.wait_ge(ts_done, g + 1)
                for q in range(8):
                    if q >= 2:
                        pe.wait_ge((rep_a, rep_v)[q % 2], g * 4 + q // 2)
                    for r in range(4):
                        s = 4 * q + r
                        last = nc.tensor.matmul(ps[:, 4 * (q % 2) + r, :], stack3[:, s:s + 1].to_broadcast([96, P]),
                                                bc_st, start=True, stop=True)
                    last.then_inc(rep_ps, 1)
                pe.wait_ge(rep_v, g * 4 + 4)
                dt_product(g * NI, g * (NI // 2), 0)
                with pe.Fori(0, NI // 2 - 1) as m:
                    sums(g * NI + m * 2, g * (NI // 2) + m, 0, True)
                    sums(g * NI + m * 2 + 1, g * (NI // 2) + m, 1, True)
                sums(g * NI + NI - 2, g * (NI // 2) + NI // 2 - 1, 0, True)
                sums(g * NI + NI - 1, g * (NI // 2) + NI // 2 - 1, 1, False)
                pe.wait_ge(y_done, (g + 1) * NI + 1)
                for b in range(GB):
                    for ic in range(NI):
                        last = nc.tensor.matmul(ps[:, b, :], gate[:, ic, b * T:(b + 1) * T], w_outp[:, ic, :],
                                                start=(ic == 0), stop=(ic == NI - 1))
                    last.then_inc(outp_ps, 1)
                with pe.Fori(0, GB) as b:
                    i = g * GB + b
                    pe.wait_ge(att_zero, (g + 1) * 3)
                    pe.wait_ge(xb_done, i + 1)
                    for j in range(4):
                        nc.tensor.matmul(ps[:, j, :], w_qk[:, j, :], xb, start=True, stop=True).then_inc(qk_ps, 1)
                    for kb in range(NB4):
                        last = nc.tensor.matmul(ps[:, 4, kb * P:(kb + 1) * P], xb[:, kb * P:(kb + 1) * P], w_v[:],
                                                start=True, stop=True)
                    last.then_inc(v_ps, 1)
                    pe.wait_ge(qk_done, i * 4 + 4)
                    for st in range(8):
                        blk, pair = st // 2, st % 2
                        lo, hi, at = window(blk)
                        bank = 2 * (st % 3)
                        if st == 2:
                            pe.wait_ge(v_done, i + 1)
                        if st >= 3:
                            pe.wait_ge(max_done, i * 8 + st - 2)
                        for a in range(2):
                            out = ps[:, bank + a, :].rearrange("p (j w) -> p j w", j=NJ)
                            nc.tensor.matmul(out[:, :, lo:hi], ident_bf[:],
                                             band[:, 0:1, lo:hi].to_broadcast([P, NJ, hi - lo]),
                                             start=True, stop=False, skip_group_check=True)
                        for j in range(NJ):
                            for a in range(2):
                                r = 32 * (2 * pair + a)
                                last = nc.tensor.matmul(
                                    ps[:, bank + a, j * WIN + lo:j * WIN + hi],
                                    qk[r:r + DH, j, blk * P:(blk + 1) * P], qk[r:r + DH, 2 + j, at:at + hi - lo],
                                    start=False, stop=True, skip_group_check=True)
                        last.then_inc(s_ps, 1)
                    pe.wait_ge(max_done, i * 8 + 8)
                    for j in range(NJ):
                        for qb in range(NB4):
                            last = nc.tensor.matmul(ps[:, 6 + j, qb * P:(qb + 1) * P], nmax[:, qb, j, :], ident[:],
                                                    start=True, stop=True)
                        last.then_inc(shift_ps, 1)
                    pe.wait_ge(q_done, i * 2 + 2)
                    for st in range(8 + 2):
                        if st < 8:
                            blk, pair = st // 2, st % 2
                            lo, hi, at = window(blk)
                            bank = 2 * (st % 3)
                            if st >= 3:
                                pe.wait_ge(p_done, i * 8 + st - 2)
                            for a in range(2):
                                out = ps[:, bank + a, :].rearrange("p (j w) -> p j w", j=NJ)
                                nc.tensor.matmul(out[:, :, lo:hi], ident_bf[:],
                                                 band[:, 1:2, lo:hi].to_broadcast([P, NJ, hi - lo]),
                                                 start=True, stop=False, skip_group_check=True)
                            for j in range(NJ):
                                for a in range(2):
                                    r = 32 * (2 * pair + a)
                                    last = nc.tensor.matmul(
                                        ps[:, bank + a, j * WIN + lo:j * WIN + hi],
                                        qk[r:r + 32, 2 + j, blk * P:(blk + 1) * P], qk[r:r + 32, j, at:at + hi - lo],
                                        start=False, stop=True, skip_group_check=True)
                            last.then_inc(st_ps, 1)
                        if st >= 2 and st % 2 == 1:
                            kb = (st - 3) // 2
                            lo, hi, at = window(kb)
                            pe.wait_ge(p_done, i * 8 + 2 * kb + 2)
                            for j in range(NJ):
                                for hp in range(4):
                                    last = nc.tensor.matmul(
                                        ps[32 * hp:32 * hp + 32, 6 + j, at:at + hi - lo],
                                        v_aug[:, kb, 4 * j + hp, :], probs[:, kb, j, hp, lo:hi],
                                        start=(kb == 0), stop=(kb == NB4 - 1), skip_group_check=True)
                    last.then_inc(o_ps, 1)
                    for j in range(NJ):
                        pe.wait_ge(o_done, i * 2 + j + 1)
                        nc.tensor.matmul(ps[:, j, :], den_sel[:], o_sb[:, j, :], start=True, stop=True).then_inc(den_ps, 1)
                    for j in range(NJ):
                        pe.wait_ge(on_done, i * 2 + j + 1)
                        last = nc.tensor.matmul(ps[:, 2, :], w_o[:, j, :], o_sb[:, j, :], start=(j == 0), stop=(j == 1))
                    last.then_inc(wo_ps, 1)
                    pe.wait_ge(enc_used, i + 2)
                    nc.tensor.matmul(ps[:, 3, :], w_ct[:], relu_o, start=True, stop=True).then_inc(ct_ps, 1)
                transposes(g, 1)
                for k in range(KH):
                    pe.wait_ge(xt_done, g * 2 * KH + KH + k + 1)
                    last = nc.tensor.matmul(ps[:, 4, :], w_down[:, k, :], xt[:, k, :], start=(k == 0), stop=(k == KH - 1))
                last.then_inc(down_ps, 1)
                for b in range(GB):
                    for k in range(KH):
                        last = nc.tensor.matmul(ps[:, 5, b * NE:(b + 1) * NE], xt[:, k, b * T:(b + 1) * T],
                                                w_router[:, k, :], start=(k == 0), stop=(k == KH - 1))
                last.then_inc(logit_ps, 1)
                pe.wait_ge(grep_done, g + 1)
                for b in range(GB):
                    last = nc.tensor.matmul(ps[:, 6, b * T:(b + 1) * T], g_rep[:, b].rearrange("p e i -> p (e i)"),
                                            ident[:], start=True, stop=True)
                last.then_inc(gt_ps, 1)
                pe.wait_ge(gated_done, g + 1)
                for b in range(GB):
                    nc.tensor.matmul(ps[:, b, :], gated[:, b * T:(b + 1) * T], w_up[:], start=True, stop=True).then_inc(up_ps, 1)

        @block.vector
        def _(dve):
            dve.wait_ge(a_exp, 1)
            dve.wait_ge(const_done, 1)
            nc.vector.tensor_scalar(a_neg[:], a_neg[:], -1.0, None, ALU.mult).then_inc(setup_done, 1)
            dve.sem_inc(h_done, H0)
            dve.sem_inc(hc_used, U0)
            dve.sem_inc(dt_ps, 2)
            dve.sem_inc(relu_dt, 2)
            dve.sem_inc(du_done, 1)
            dve.sem_inc(dt_done, 1)
            dve.sem_inc(y_done, 1)
            dve.sem_inc(enc_used, 1)
            dve.sem_inc(x_out, 1)
            nc.vector.tensor_scalar(b_qk[:, 0:NJ], b_qk[:, 0:NJ], 0.25, None, ALU.mult).then_inc(setup_done, 1)

            def hold():
                nc.vector.tensor_copy(held[:], neg_half[:, 0:1])

            def norm_stats(g, use):
                n = g * 3 + use
                for b in range(GB):
                    nc.vector.bn_stats(ln_st[:, b, :], x[:, b, :]).then_inc(ln_stat, 1)
                dve.wait_ge(ln_stat, (n + 1) * GB)
                hold()
                for b in range(GB):
                    nc.vector.bn_aggr(ln_mv[:, b, :], ln_st[:, b, :]).then_inc(ln_aggr, 1)
                dve.wait_ge(ln_aggr, (n + 1) * GB)
                nc.vector.tensor_scalar(ln_rs[:], ln_mv[:, :, 1], EPS, None, ALU.add).then_inc(ln_eps, 1)
                dve.wait_ge(ln_rstd, n + 1)

            def norm_all(g, use):
                norm_stats(g, use)
                for b in range(GB):
                    nc.vector.tensor_scalar(xn[:, b, :], x[:, b, :], ln_mv[:, b, 0:1], ln_rs[:, b:b + 1],
                                            ALU.subtract, ALU.mult).then_inc(ln_out, 1)

            def soft_step(s, c, ic, p):
                if s == 0:
                    dve.wait_ge(sp_exp, c + 1)
                    dve.wait_ge(dt_done, c + 1)
                    nc.vector.tensor_scalar(tmp[:], soft[:], 1.0, 1.0, ALU.add, ALU.subtract).then_inc(sp_r, 1)
                elif s == 1:
                    dve.wait_ge(sp_r, c + 1)
                    nc.vector.tensor_tensor(tmp[:], soft[:], tmp[:], ALU.subtract).then_inc(sp_c, 1)
                elif s == 2:
                    dve.wait_ge(sp_c, c + 1)
                    dve.wait_ge(sp_ln, c + 1)
                    nc.vector.tensor_tensor(delta[:, p, :], delta[:, p, :], tmp[:], ALU.add).then_inc(sp_d, 1)
                elif s == 3:
                    dve.wait_ge(sp_d, c + 1)
                    nc.vector.tensor_scalar(tmp[:], ps[:, 6 + p, :], dt_b[:, bass.ds(ic, 1)], 0.0, ALU.add,
                                            ALU.max).then_inc(relu_dt, 1)
                elif s == 4:
                    dve.wait_ge(relu_dt, c + 3)
                    nc.vector.tensor_tensor(delta[:, p, :], delta[:, p, :], tmp[:], ALU.add).then_inc(dt_done, 1)
                elif s == 5:
                    dve.wait_ge(dt_done, c + 2)
                    nc.vector.tensor_tensor(du[:, p, :], delta[:, p, :], u[:, bass.ds(ic, 1), :], ALU.mult).then_inc(du_done, 1)

            def times_c(c, n):
                dve.wait_ge(h_done, H0 + 1 + c * N + n)
                nc.vector.tensor_tensor(ring[:, n % RING, :], ring[:, n % RING, :], bc[:, N + n, :],
                                        ALU.mult).then_inc(hcd_done, 1)

            def scans(c, ic, p, ahead):
                for n in range(N):
                    dve.wait_ge(da_done, c * N + n + 1)
                    dve.wait_ge(dbx_done, c * N + n + 1)
                    nc.vector.tensor_tensor_scan(ring[:, n % RING, :], ps[:, n % DAR, :], ring[:, n % RING, :], 0.0,
                                                 ALU.mult, ALU.add).then_inc(h_done, 1)
                    if n and n - 1 not in POOL_C:
                        times_c(c, n - 1)
                    if ahead and 7 <= n < 13:
                        soft_step(n - 7, c + 1, ic + 1, 1 - p)
                times_c(c, N - 1)
                dve.wait_ge(hc_used, U0 + (c + 1) * N)
                dve.wait_ge(y_done, c + 1)
                nc.vector.scalar_tensor_tensor(y_tmp[:], u[:, bass.ds(ic, 1), :], d_skip[:, bass.ds(ic, 1)], ps[:, 4 + p, :],
                                               ALU.mult, ALU.add).then_inc(y_sum, 1)
                dve.wait_ge(y_sum, c + 1)
                nc.vector.tensor_tensor(gate[:, bass.ds(ic, 1), :], y_tmp[:], gate[:, bass.ds(ic, 1), :], ALU.mult).then_inc(y_done, 1)

            def chain(i, k):
                dve.wait_ge(small_done, i * NSMALL + k)

            with dve.Fori(0, NG) as g:
                dve.wait_ge(x_in, (g + 1) * 16)
                norm_all(g, 0)
                for ic in range(NI):
                    acc = hc0[:, ic % 2, :].rearrange("p (b t) -> p b t", b=GB)
                    src = ps[:, 4 + ic % 2, :].rearrange("p (b t) -> p b t", b=GB)
                    dve.wait_ge(tap3_done, g * NI + ic + 1)
                    for s in range(1, KC):
                        if s > 1:
                            dve.wait_ge(tap_done, (g * NI + ic) * 2 + s - 1)
                        nc.vector.scalar_tensor_tensor(acc[:, :, s:T], src[:, :, 0:T - s],
                                                       conv_w[:, ic, KC - 1 - s:KC - s], acc[:, :, s:T],
                                                       ALU.mult, ALU.add).then_inc(tap_done if s < KC - 1 else conv_done, 1)
                dve.wait_ge(bc_ps, g + 1)
                nc.vector.tensor_copy(bc_hi, ps[0:96, 1, :]).then_inc(split_done, 1)
                dve.wait_ge(split_done, g * 6 + 1)
                nc.vector.tensor_tensor(bc_r1, ps[0:96, 1, :], bc_hi, ALU.subtract).then_inc(split_done, 1)
                dve.wait_ge(split_done, g * 6 + 2)
                nc.vector.tensor_copy(bc_mid, bc_r1).then_inc(split_done, 1)
                nc.vector.tensor_copy(bc_st[0:32], bc_hi[0:32])
                dve.wait_ge(split_done, g * 6 + 3)
                nc.vector.tensor_tensor(bc_r2, bc_r1, bc_mid, ALU.subtract).then_inc(split_done, 1)
                nc.vector.tensor_copy(bc_st[32:64], bc_mid[32:64]).then_inc(split_done, 1)
                dve.wait_ge(split_done, g * 6 + 5)
                nc.vector.tensor_copy(bc_st[64:96], bc_r2[64:96]).then_inc(split_done, 1)
                for q in range(1, 8, 2):
                    dve.wait_ge(rep_ps, g * 8 + q + 1)
                    nc.vector.tensor_copy(bc[:, 4 * q:4 * q + 4, :], ps[:, 4:8, :]).then_inc(rep_v, 1)
                dve.wait_ge(rep_a, g * 4 + 4)
                nc.vector.memset(ps[:, 0:DAR, :].rearrange("p s (b t) -> p s b t", b=GB)[:, :, :, 0:1], 0.0).then_inc(da_zeroed, 1)
                for s in range(6):
                    soft_step(s, g * NI, 0, 0)
                with dve.Fori(0, NI // 2 - 1) as m:
                    scans(g * NI + m * 2, m * 2, 0, True)
                    scans(g * NI + m * 2 + 1, m * 2 + 1, 1, True)
                scans(g * NI + NI - 2, NI - 2, 0, True)
                scans(g * NI + NI - 1, NI - 1, 1, False)
                for b in range(GB):
                    dve.wait_ge(outp_ps, g * GB + b + 1)
                    nc.vector.tensor_tensor(x[:, b, :], ps[:, b, :], x[:, b, :], ALU.add).then_inc(x1_done, 1)
                dve.wait_ge(x1_done, (g + 1) * GB)
                norm_stats(g, 1)
                hold()
                with dve.Fori(0, GB) as b:
                    i = g * GB + b
                    nc.vector.tensor_scalar(xb, x[:, bass.ds(b, 1), :], ln_mv[:, bass.ds(b, 1), 0], ln_rs[:, bass.ds(b, 1)],
                                            ALU.subtract, ALU.mult).then_inc(xb_done, 1)
                    dve.wait_ge(att_zero, (g + 1) * 3)
                    dve.wait_ge(v_ps, i + 1)
                    nc.vector.tensor_copy(v_aug[:, :, :, 0:DH].rearrange("p k h d -> p (k h) d"),
                                          ps[:, 4, :].rearrange("p (a d) -> p a d", d=DH)).then_inc(v_done, 1)
                    for st in range(8):
                        blk, pair = st // 2, st % 2
                        lo, hi, _ = window(blk)
                        bank = 2 * (st % 3)
                        dve.wait_ge(s_ps, i * 8 + st + 1)
                        dst = nmax[:, blk].rearrange("p j (a r) -> p a j r", r=32)[:, 2 * pair:2 * pair + 2, :, DH]
                        nc.vector.tensor_reduce(
                            dst, ps[:, bank:bank + 2, :].rearrange("p a (j w) -> p a j w", j=NJ)[:, :, :, lo:hi],
                            AX.X, ALU.max, negate=True).then_inc(max_done, 1)
                    for j in range(NJ):
                        dve.wait_ge(shift_ps, i * 2 + j + 1)
                        nc.vector.tensor_tensor(qk[:, j, :], ps[:, 6 + j, :], qk[:, j, :], ALU.add).then_inc(q_done, 1)
                    for j in range(NJ):
                        dve.wait_ge(den_ps, i * 2 + j + 1)
                        nc.vector.reciprocal(rden[:, j, :], ps[:, j, :]).then_inc(rden_done, 1)
                    for j in range(NJ):
                        dve.wait_ge(rden_done, i * 2 + j + 1)
                        nc.vector.tensor_tensor(o_sb[:, j, :], o_sb[:, j, :], rden[:, j, :], ALU.mult).then_inc(on_done, 1)
                    dve.wait_ge(enc_in, (i + 1) * 16)
                    dve.wait_ge(relu_done, i + 1)
                    nc.vector.tensor_tensor(relu_o, relu_o, enc, ALU.mult).then_inc(enc_used, 1)
                    dve.wait_ge(ct_ps, i + 1)
                    nc.vector.scalar_tensor_tensor(x[:, bass.ds(b, 1), :], ps[:, 3, :], b_ct[:], x[:, bass.ds(b, 1), :],
                                                   ALU.add, ALU.add).then_inc(x2_done, 1)
                dve.wait_ge(x2_done, (g + 1) * GB)
                norm_all(g, 2)
                lg = small[:, 0:32].rearrange("p (b e) -> p b e", b=GB)
                top = small[:, 32:64].rearrange("p (b e) -> p b e", b=GB)
                ex = small[:, 64:96].rearrange("p (b e) -> p b e", b=GB)
                tot, rtot = small[:, 96:100], small[:, 100:104]
                idx = small[:, 128:160].bitcast(U32).rearrange("p (b e) -> p b e", b=GB)
                idf = small[:, 160:168].rearrange("p (b s) -> p b s", b=GB)
                eq = small[:, 192:256].rearrange("p (b s e) -> p b s e", b=GB, s=2)
                wt = small[:, 256:288].rearrange("p (b e) -> p b e", b=GB)
                dve.wait_ge(logit_ps, g + 1)
                nc.vector.tensor_copy(lg, ps[:, 5, 0:GB * NE].rearrange("p (b e) -> p b e", b=GB)).then_inc(small_done, 1)
                chain(g, 1)
                hold()
                for b in range(GB):
                    nc.vector.max(top[:, b, :], lg[:, b, :]).then_inc(small_done, 1)
                chain(g, 5)
                nc.vector.tensor_tensor(ex, lg, top[:, :, 0:1].to_broadcast([P, GB, NE]), ALU.subtract).then_inc(small_done, 1)
                dve.wait_ge(lexp_done, g + 1)
                nc.vector.tensor_reduce(tot, ex, AX.X, ALU.add).then_inc(small_done, 1)
                chain(g, 7)
                nc.vector.reciprocal(rtot, tot).then_inc(small_done, 1)
                chain(g, 8)
                nc.vector.tensor_tensor(wt, ex, rtot.rearrange("p (b o) -> p b o", o=1).to_broadcast([P, GB, NE]),
                                        ALU.mult).then_inc(small_done, 1)
                chain(g, 9)
                hold()
                for b in range(GB):
                    nc.vector.max(top[:, b, :], wt[:, b, :])
                nc.vector.tensor_copy(lg, wt).then_inc(small_done, 1)
                chain(g, 10)
                hold()
                for b in range(GB):
                    nc.vector.max_index(idx[:, b, :], top[:, b, :], wt[:, b, :])
                nc.vector.tensor_copy(lg, wt).then_inc(small_done, 1)
                chain(g, 11)
                nc.vector.tensor_copy(idf, idx[:, :, 0:2]).then_inc(small_done, 1)
                chain(g, 12)
                for s in range(2):
                    last = nc.vector.tensor_tensor(
                        eq[:, :, s, :], iota[:].rearrange("p (o e) -> p o e", o=1).to_broadcast([P, GB, NE]),
                        idf[:, :, s:s + 1].to_broadcast([P, GB, NE]), ALU.is_equal)
                last.then_inc(small_done, 1)
                chain(g, 13)
                nc.vector.tensor_tensor(eq[:, :, 0, :], eq[:, :, 0, :], eq[:, :, 1, :], ALU.add).then_inc(gate_step, 1)
                dve.wait_ge(gate_step, g * 2 + 1)
                nc.vector.tensor_tensor(wt, wt, eq[:, :, 0, :], ALU.mult).then_inc(gate_step, 1)
                dve.wait_ge(gate_step, g * 2 + 2)
                nc.vector.tensor_copy(g_rep, small[:, 256:288].rearrange("p (b e o) -> p b e o", b=GB, o=1)
                                      .to_broadcast([P, GB, NE, 16])).then_inc(grep_done, 1)
                dve.wait_ge(gt_ps, g + 1)
                dve.wait_ge(act_done, g + 1)
                nc.vector.tensor_tensor(gated, ps[:, 6, :], act_e, ALU.mult).then_inc(gated_done, 1)
                for b in range(GB):
                    dve.wait_ge(up_ps, g * GB + b + 1)
                    nc.vector.tensor_tensor(x[:, b, :], ps[:, b, :], x[:, b, :], ALU.add).then_inc(x3_done, 1)


def kernel(**inputs):
    import numpy as np
    import ml_dtypes
    import concourse.bacc as bacc
    from concourse.bass_utils import run_bass_kernel_spmd

    a = {k: np.asarray(v) for k, v in inputs.items()}
    P, DH, NHEAD, NJ = 128, 16, 8, 2

    def chunks(w):
        return np.ascontiguousarray(np.swapaxes(w.reshape(-1, P, *w.shape[1:]), 0, 1))

    def pad_heads(w, axis_first):
        out = np.zeros((NJ, 4, 32) + w.shape[1:], np.float32)
        out[:, :, :DH] = w.reshape((NJ, 4, DH) + w.shape[1:])
        return out.reshape((NJ, P) + w.shape[1:])

    w_in, b_in = a["L0_xattn_w_in"], a["L0_xattn_b_in"]
    xp = a["L0_attn_x_proj_w"].T
    w_qk = np.concatenate([pad_heads(w_in[0:P], 0), pad_heads(w_in[P:2 * P], 0)])
    b_qk = np.concatenate([pad_heads(b_in[0:P], 0), pad_heads(b_in[P:2 * P], 0)]).T.copy()
    b_qk.reshape(4, 32, 4)[:, DH, 2:4] = 1.0
    row, col = np.arange(P)[:, None], np.arange(2 * P)[None, :]
    outside = np.abs(col - 64 - row) > 64
    band = np.zeros((P, 2, 2 * P), np.float32)
    band[:, 0][outside] = -1e37
    band[:, 1][outside] = -1e37
    den = np.zeros((P, P), np.float32)
    for hp in range(4):
        den[32 * hp + DH, 32 * hp:32 * hp + 32] = 1.0
    bf = ml_dtypes.bfloat16
    f = np.ascontiguousarray
    feeds = {
        "x": a["x"], "ctx": a["ctx_2048"],
        "w_in": chunks(a["L0_attn_in_proj_w"].T),
        "conv_w": chunks(a["L0_attn_conv_w"][:, 0, :]), "conv_b": chunks(a["L0_attn_conv_b"]),
        "w_xt": chunks(xp[:, 0:P]), "w_xbc": chunks(np.tile(xp[:, P:], (1, 3))),
        "w_dt": f(a["L0_attn_dt_proj_w"].T), "dt_b": chunks(a["L0_attn_dt_proj_b"]),
        "a_log": chunks(a["L0_attn_A_log"]), "d_skip": chunks(a["L0_attn_D"]),
        "w_outp": chunks(a["L0_attn_out_proj_w"].T),
        "w_qk": f(w_qk.transpose(2, 0, 1)), "b_qk": f(b_qk),
        "w_v": f(w_in[2 * P:].T), "b_v": f(pad_heads(b_in[2 * P:], 0).T),
        "w_o": f(pad_heads(a["L0_xattn_w_out"].T, 0).transpose(1, 0, 2)), "b_o": a["L0_xattn_b_out"].reshape(P, 1),
        "w_ct": a["L0_xattn_w_ct"], "b_ct": a["L0_xattn_b_ct"].reshape(P, 1),
        "w_router": chunks(a["L0_ffn_router_w"].T),
        "w_down": chunks(a["L0_ffn_down_w"].reshape(P, -1).T),
        "w_up": f(a["L0_ffn_up_w"].transpose(0, 2, 1).reshape(P, -1)),
        "ident": np.eye(P, dtype=np.float32), "ident_bf": np.eye(P).astype(bf), "band": band.astype(bf),
        "stack": np.tile(np.eye(32), (3, 1)).astype(bf), "den": den,
        "iota": np.tile(np.arange(8, dtype=np.float32), (P, 1)),
    }
    nc = bacc.Bacc("TRN2", target_bir_lowering=False, num_devices=1)
    aps = [nc.dram_tensor(f"in_{k}", v.shape, mybir.dt.from_np(v.dtype), kind="ExternalInput").ap()
           for k, v in feeds.items()]
    out = nc.dram_tensor("out", a["x"].shape, mybir.dt.float32, kind="ExternalOutput").ap()
    decoder_layer(nc, *aps, out)
    r = run_bass_kernel_spmd(nc, [{f"in_{k}": v for k, v in feeds.items()}], core_ids=[0])
    return r.results[0]["out"]
```

```python
import concourse.bass as bass
from concourse import mybir
from contextlib import ExitStack


def decoder_layer(nc, x_d, ctx_d, w_in_d, conv_w_d, conv_b_d, w_xt_d, w_xbc_d, w_dt_d, dt_b_d, a_log_d,
                  d_skip_d, w_outp_d, w_qk_d, b_qk_d, w_v_d, b_v_d, w_o_d, b_o_d, w_ct_d, b_ct_d,
                  w_router_d, w_down_d, w_up_d, ident_d, ident_bf_d, band_d, stack_d, den_d, iota_d, out_d):
    F32, BF, U32 = mybir.dt.float32, mybir.dt.bfloat16, mybir.dt.uint32
    ALU, ACT, AX = mybir.AluOpType, mybir.ActivationFunctionType, mybir.AxisListType

    P = 128
    B, T, H = x_d.shape
    GB = 2
    NG = B // GB
    NT = GB * T
    KH = H // P
    I = w_outp_d.shape[1] * P
    NI = I // P
    NQ = NI // 2
    N = a_log_d.shape[2]
    KC = conv_w_d.shape[2]
    NHEAD, DH = 8, 16
    NJ = 2
    NE = w_router_d.shape[2]
    EPS = 1e-5
    NBLK = H // P
    WIN = 2 * P
    RS = N // 2
    SB = RS * NI // GB
    SG = RS * NI
    RING = 8
    DAR = 2
    POOL_C = (1, 4, 6)
    NPC = len(POOL_C)
    NDC = RS - NPC
    BATCH = 2
    LAG = 1
    PS_Y, PS_ATT = 2, 4

    stack = ExitStack()
    with stack:
        def sb(name, shape, dt=F32):
            return stack.enter_context(nc.sbuf_tensor(name, shape, dt))

        def sem(name):
            return stack.enter_context(nc.semaphore(name))

        w_in = sb("w_in", [P, KH, 2 * I])
        conv_w = sb("conv_w", [P, NI, KC])
        conv_b = sb("conv_b", [P, NI])
        w_xt = sb("w_xt", [P, NI, P])
        w_xbc = sb("w_xbc", [P, NI, 96])
        w_dt = sb("w_dt", [P, I])
        dt_b = sb("dt_b", [P, NI])
        a_neg = sb("a_neg", [P, NI, N])
        d_skip = sb("d_skip", [P, NI])
        w_outp = sb("w_outp", [P, NI, H])
        w_qk = sb("w_qk", [P, 4, P])
        b_qk = sb("b_qk", [P, 4])
        w_v = sb("w_v", [P, P])
        b_v = sb("b_v", [P, NJ])
        w_o = sb("w_o", [P, NJ, P])
        b_o = sb("b_o", [P, 1])
        w_ct = sb("w_ct", [P, P])
        b_ct = sb("b_ct", [P, 1])
        w_router = sb("w_router", [P, KH, NE])
        w_down = sb("w_down", [P, KH, P])
        w_up = sb("w_up", [P, H])
        ident = sb("ident", [P, P])
        ident_bf = sb("ident_bf", [P, P], BF)
        band = sb("band", [P, 1, WIN], BF)
        stack3 = sb("stack3", [96, 32], BF)
        den_sel = sb("den_sel", [P, NHEAD // NJ])
        iota = sb("iota", [P, NE])
        neg_half = sb("neg_half", [P, GB])
        held = sb("held", [P, 1])
        x_res = sb("x_res", [P, GB, H])
        u = sb("u", [P, NI, NT])
        gate = sb("gate", [P, NI, NT])
        ring = sb("ring", [P, RING, 2 * NT])
        delta = sb("delta", [P, NI, NT])
        du = sb("du", [P, 2, 2 * NT])
        soft = sb("soft", [P, 2 * NT])
        tmp = sb("tmp", [P, 2 * NT])
        pos = sb("pos", [P, 2 * NT])
        y_tmp = sb("y_tmp", [P, NT])
        ts = sb("ts", [P, NT])
        shared = sb("shared", [P, 2 * N * NT])
        x_att = sb("x_att", [P, GB, H])
        probs_mem = sb("probs_mem", [P, 4 * 4 * WIN])
        qk = sb("qk", [P, 4, H])
        o_sb = sb("o_sb", [P, NJ, H])
        rden = sb("rden", [P, NBLK * NHEAD])
        xb = sb("xb", [P, H])
        enc = sb("enc", [P, H])
        v_aug = sb("v_aug", [P, NBLK, NHEAD, 32])
        nmax = sb("nmax", [P, NBLK, NJ, P])
        ln_st = {k: sb("ln_st_" + k, [P, GB, 6]) for k in "ate"}
        ln_mv = {k: sb("ln_mv_" + k, [P, GB, 2]) for k in "ate"}
        ln_rs = {k: sb("ln_rs_" + k, [P, GB]) for k in "ate"}
        small = sb("small", [P, 8 * 16 * GB])

        def part(mem, at, *dims):
            size = 1
            for d in dims:
                size *= d
            v = mem[:, at:at + size]
            if len(dims) == 1:
                return v
            names = "abcd"[:len(dims)]
            return v.rearrange("p (" + " ".join(names) + ") -> p " + " ".join(names),
                               **dict(zip(names, dims)))

        bc = part(shared, 0, 2 * N, NT)
        xn_a = part(shared, 0, GB, H)
        xt_a = part(shared, GB * H, KH, NT)
        hc0 = part(shared, 2 * GB * H, 4, NT)
        probs = part(probs_mem, 0, 4, NBLK, WIN)
        rden_rep = part(probs_mem, 0, NBLK * NHEAD * 32)
        xn_e = part(probs_mem, 0, GB, H)
        xt_e = part(probs_mem, GB * H, KH, NT)
        act_e = part(probs_mem, 2 * GB * H, NT)
        gated = part(probs_mem, 2 * GB * H + NT, NT)
        g_rep = part(probs_mem, 2 * GB * H + 2 * NT, GB, NE, 16)
        x_new = ring[:, 0:2, :].rearrange("p s (k c) -> p (s k c)", k=1).rearrange("p (b h) -> p b h", b=GB)
        bc_hi = ring[0:96, 2, 0:NT // 2].bitcast(BF)
        bc_mid = ring[0:96, 3, 0:NT // 2].bitcast(BF)
        bc_r1 = ring[0:96, 4, 0:NT]
        bc_r2 = ring[0:96, 5, 0:NT]
        bc_st = ring[0:96, 6, 0:NT // 2].bitcast(BF)

        ps = stack.enter_context(nc.psum_tensor("ps", [P, 8, 512], F32))

        w_loaded = sem("w_loaded")
        x_in, xres_in, x_out, enc_in = sem("x_in"), sem("xres_in"), sem("x_out"), sem("enc_in")
        const_done, setup_done, a_exp = sem("const_done"), sem("setup_done"), sem("a_exp")
        bo_ps, bo_done, att_zero = sem("bo_ps"), sem("bo_done"), sem("att_zero")
        ln_stat, ln_aggr, ln_eps, ln_rstd, ln_out = [
            {k: sem(f"{what}_{k}") for k in "ate"} for what in ("ln_stat", "ln_aggr", "ln_eps", "ln_rstd", "ln_out")]
        xt_ps = {k: sem("xt_ps_" + k) for k in "ae"}
        xt_done = {k: sem("xt_done_" + k) for k in "ae"}
        hin_ps, gin_ps, tap3_done, tap_done, conv_done, u_done, gate_done = [
            sem(k) for k in ("hin_ps", "gin_ps", "tap3_done", "tap_done", "conv_done", "u_done", "gate_done")]
        ts_ps, ts_done, bc_ps, split_done = [sem(k) for k in ("ts_ps", "ts_done", "bc_ps", "split_done")]
        rep_ps, rep_a, rep_v, da_zeroed = [sem(k) for k in ("rep_ps", "rep_a", "rep_v", "da_zeroed")]
        dt_ps, z_done, sp_abs, sp_exp, sp_ln, sp_r, sp_pos, sp_c, sp_d, dt_done, du_done = [
            sem(k) for k in ("dt_ps", "z_done", "sp_abs", "sp_exp", "sp_ln", "sp_r", "sp_pos", "sp_c", "sp_d",
                             "dt_done", "du_done")]
        da_done, dbx_done, h_done, hcd_done, hcp_done, hc_used = [
            sem(k) for k in ("da_done", "dbx_done", "h_done", "hcd_done", "hcp_done", "hc_used")]
        y_sum, y_done, outp_ps, x1_done, x1_copied = [
            sem(k) for k in ("y_sum", "y_done", "outp_ps", "x1_done", "x1_copied")]
        xb_done, qk_ps, qk_done, v_ps, v_done = [sem(k) for k in ("xb_done", "qk_ps", "qk_done", "v_ps", "v_done")]
        s_ps, max_done, shift_ps, q_done, st_ps, p_done, o_ps, o_done = [
            sem(k) for k in ("s_ps", "max_done", "shift_ps", "q_done", "st_ps", "p_done", "o_ps", "o_done")]
        den_ps, rden_done, rden_wide, rrep_ps, on_done, wo_ps, relu_done, enc_used, ct_ps, x2_done = [
            sem(k) for k in ("den_ps", "rden_done", "rden_wide", "rrep_ps", "on_done", "wo_ps", "relu_done", "enc_used", "ct_ps", "x2_done")]
        down_ps, act_done, logit_ps, small_done, lexp_done, gate_step, grep_done, gt_ps, gated_done, up_ps, x3_done = [
            sem(k) for k in ("down_ps", "act_done", "logit_ps", "small_done", "lexp_done", "gate_step", "grep_done",
                             "gt_ps", "gated_done", "up_ps", "x3_done")]

        H0 = DAR
        U0 = RING
        NSMALL = 13 - 4 + GB

        resident = [(w_in, w_in_d), (conv_w, conv_w_d), (conv_b, conv_b_d), (w_xt, w_xt_d),
                    (w_xbc, w_xbc_d), (w_dt, w_dt_d), (dt_b, dt_b_d), (a_neg, a_log_d), (d_skip, d_skip_d),
                    (w_outp, w_outp_d), (w_qk, w_qk_d), (b_qk, b_qk_d), (w_v, w_v_d), (b_v, b_v_d),
                    (w_o, w_o_d), (b_o, b_o_d), (w_ct, w_ct_d), (b_ct, b_ct_d), (w_router, w_router_d),
                    (w_down, w_down_d), (w_up, w_up_d), (ident, ident_d), (ident_bf, ident_bf_d),
                    (band, band_d), (stack3, stack_d), (den_sel, den_d), (iota, iota_d)]
        ALL_W = 16 * len(resident)

        def window(blk):
            lo = 64 if blk == 0 else 0
            hi = WIN - 64 if blk == NBLK - 1 else WIN
            return lo, hi, blk * P - 64 + lo

        def dpc(r):
            return len([a for a in range(r) if a not in POOL_C])

        PE_AT = {0: ("proj",), 3: ("s", 0), 5: ("s", 1), 7: ("s", 2), 9: ("s", 3), 11: ("shift",),
                 12: ("st", 0), 14: ("st", 1), 16: ("av", 0), 18: ("st", 2), 20: ("st", 3), 22: ("av", 1),
                 23: ("den",), 25: ("rep",), 27: ("wo",), 29: ("ct",)}
        ACT_AT = {4: ("qk",), 15: ("exp", 0), 17: ("exp", 1), 19: ("o", 0), 21: ("exp", 2), 23: ("exp", 3),
                  24: ("o", 1), 25: ("wide",), 29: ("relu",)}
        DVE_AT = {0: ("xb",), 3: ("v",), 5: ("max", 0), 7: ("max", 1), 9: ("max", 2), 11: ("max", 3),
                  13: ("addq",), 24: ("rden",), 26: ("on",), 29: ("enc",), 30: ("x2",)}

        SOFT_AT = {3: -2, 7: -1, 8: 0, 9: 1, 10: 2, 11: 3}

        block = stack.enter_context(nc.Block())

        @block.sync
        def _(sp):
            for dst, src in resident:
                sp.dma_start(dst[:], src).then_inc(w_loaded, 16)

            def rows(dram, g):
                return dram[bass.ds(g * GB, GB)].rearrange("b t h -> t b h")

            def contexts(g):
                for b in range(GB):
                    i = g * GB + b
                    sp.wait_ge(enc_used, i + 1)
                    sp.dma_start(enc[:], ctx_d[i]).then_inc(enc_in, 16)

            def store(g):
                sp.wait_ge(x3_done, (g + 1) * GB)
                sp.dma_start(rows(out_d, g), x_att[:]).then_inc(x_out, 16)

            def load_next(g):
                sp.wait_ge(hc_used, U0 + (g + 1) * SG)
                sp.dma_start(x_new, rows(x_d, g + 1)).then_inc(x_in, 16)

            def load_residual(g):
                sp.wait_ge(x1_copied, g + 1)
                sp.dma_start(x_res[:], rows(x_d, g + 1)).then_inc(xres_in, 16)

            sp.dma_start(x_new, rows(x_d, 0)).then_inc(x_in, 16)
            sp.dma_start(x_res[:], rows(x_d, 0)).then_inc(xres_in, 16)
            load_next(0)
            load_residual(0)
            with sp.Fori(1, NG - 1) as g:
                contexts(g - 1)
                load_next(g)
                store(g - 1)
                load_residual(g)
            contexts(NG - 2)
            store(NG - 2)
            contexts(NG - 1)
            store(NG - 1)
            sp.wait_ge(x_out, NG * 16)

        @block.gpsimd
        def _(pool):
            nc.gpsimd.memset(neg_half[:], -0.5).then_inc(const_done, 1)
            nc.gpsimd.memset(v_aug[:, :, :, DH + 1:32], 0.0).then_inc(att_zero, 1)
            nc.gpsimd.memset(v_aug[:, :, :, DH:DH + 1], 1.0).then_inc(att_zero, 1)
            nc.gpsimd.memset(nmax[:], 0.0).then_inc(att_zero, 1)
            pool.wait_ge(const_done, 1)

            def rstd(use, j):
                pool.wait_ge(ln_eps[use], j + 1)
                nc.gpsimd.tensor_tensor(ln_rs[use][:], ln_rs[use][:], neg_half[:], ALU.pow).then_inc(ln_rstd[use], 1)

            def times_c(g, s):
                r = s % RS
                pool.wait_ge(h_done, H0 + 1 + g * SG + s)
                nc.gpsimd.tensor_tensor(ring[:, s % RING, :], ring[:, s % RING, :],
                                        bc[:, N + 2 * r:N + 2 * r + 2, :].rearrange("p a t -> p (a t)"),
                                        ALU.mult).then_inc(hcp_done, 1)

            def scans(g):
                pool.wait_ge(rep_a, (g + 1) * 4)
                pool.wait_ge(rep_v, (g + 1) * 4)
                for s in range(SG):
                    ic, r = s // RS, s % RS
                    q = ic // 2
                    if s % (2 * RS) == 0:
                        pool.wait_ge(du_done, g * NQ + q + 1)
                    pool.wait_ge(hc_used, g * SG + s + 1)
                    nc.gpsimd.tensor_tensor(
                        ring[:, s % RING, :].rearrange("p (n t) -> p n t", n=2),
                        du[:, q % 2, (ic % 2) * NT:(ic % 2 + 1) * NT].rearrange("p (n t) -> p n t", n=1)
                        .to_broadcast([P, 2, NT]),
                        bc[:, 2 * r:2 * r + 2, :], ALU.mult).then_inc(dbx_done, 1)
                    if s >= LAG and (s - LAG) % RS in POOL_C:
                        times_c(g, s - LAG)

            def projections(g):
                rstd("a", g)

            projections(0)
            scans(0)
            projections(1)
            rstd("t", 0)
            with pool.Fori(1, NG - 1) as g:
                scans(g)
                rstd("e", g - 1)
                rstd("a", g + 1)
                rstd("t", g)
            scans(NG - 1)
            rstd("e", NG - 2)
            rstd("t", NG - 1)
            rstd("e", NG - 1)

        @block.scalar
        def _(act):
            act.wait_ge(w_loaded, ALL_W)
            nc.scalar.activation(a_neg[:], a_neg[:], ACT.Exp).then_inc(a_exp, 1)
            act.wait_ge(bo_ps, 1)
            nc.scalar.activation(b_o[:], ps[:, 0, 0:1], ACT.Identity, bias=b_o[:]).then_inc(bo_done, 1)
            act.wait_ge(bo_done, 1)
            act.wait_ge(setup_done, 2)

            def transposed(use, j, xt, bank):
                for k in range(2):
                    act.wait_ge(xt_ps[use], j * 2 + k + 1)
                    nc.scalar.copy(xt[:, 2 * k:2 * k + 2, :].rearrange("p a t -> p (a t)"), ps[:, bank + k, :]).then_inc(xt_done[use], 1)

            def soft_parts(pq, q):
                z = delta[:, 2 * q:2 * q + 2, :].rearrange("p a t -> p (a t)")
                act.wait_ge(dt_done, pq + 1)
                nc.scalar.activation(soft[:], z, ACT.Abs).then_inc(sp_abs, 1)
                act.wait_ge(sp_abs, pq + 1)
                nc.scalar.activation(soft[:], soft[:], ACT.Exp, scale=-1.0).then_inc(sp_exp, 1)
                act.wait_ge(sp_exp, pq + 1)
                act.wait_ge(sp_pos, pq + 1)
                nc.scalar.activation(z, soft[:], ACT.Ln, bias=1.0).then_inc(sp_ln, 1)

            def attention_part(i, what, n=0):
                if what == "qk":
                    for j in range(4):
                        act.wait_ge(qk_ps, i * 4 + j + 1)
                        nc.scalar.activation(qk[:, j, :], ps[:, PS_ATT + j, :], ACT.Identity,
                                             scale=0.25 if j < 2 else 1.0, bias=b_qk[:, j:j + 1]).then_inc(qk_done, 1)
                elif what == "exp":
                    for a in range(2):
                        blk = 2 * (n % 2) + a
                        lo, hi, _ = window(blk)
                        act.wait_ge(st_ps, i * 4 + n + 1)
                        nc.scalar.activation(probs[:, :, blk, lo:hi], ps[:, PS_ATT:PS_ATT + 4, a * WIN + lo:a * WIN + hi],
                                             ACT.Exp).then_inc(p_done, 1)
                elif what == "o":
                    act.wait_ge(o_ps, i * 2 + n + 1)
                    nc.scalar.copy(o_sb[:, n, :], ps[:, PS_ATT, :]).then_inc(o_done, 1)
                elif what == "wide":
                    act.wait_ge(rden_done, i + 1)
                    nc.scalar.copy(rden_rep.rearrange("p (a r) -> p a r", r=32),
                                   rden[:].rearrange("p (a r) -> p a r", r=1).to_broadcast([P, NBLK * NHEAD, 32])).then_inc(rden_wide, 1)
                else:
                    act.wait_ge(wo_ps, i + 1)
                    nc.scalar.activation(xb[:], ps[:, PS_ATT + 3, :], ACT.Relu, bias=b_o[:]).then_inc(relu_done, 1)

            def scans(g, att, scan=True):
                for s in range(SG):
                    ic, r = s // RS, s % RS
                    if scan:
                        if s % (2 * RS) == 0:
                            act.wait_ge(dt_done, g * NQ + ic // 2 + 2)
                        act.wait_ge(h_done, g * SG + s + 1)
                        for n in (2 * r, 2 * r + 1):
                            nc.scalar.activation(
                                ps[:, s % DAR, (n % 2) * NT:(n % 2 + 1) * NT].rearrange("p (b t) -> p b t", b=GB)[:, :, 1:T],
                                delta[:, ic, :].rearrange("p (b t) -> p b t", b=GB)[:, :, 1:T], ACT.Exp,
                                scale=a_neg[:, ic, n:n + 1]).then_inc(da_done, 1)
                        if s % (2 * RS) == 5 and ic // 2 < NQ - 1:
                            soft_parts(g * NQ + ic // 2 + 1, ic // 2 + 1)
                    if att and s % SB in ACT_AT:
                        attention_part((g - 1) * GB + s // SB, *ACT_AT[s % SB])

            def experts_silu(g):
                act.wait_ge(down_ps, g)
                nc.scalar.activation(act_e, ps[:, 4, 0:NT], ACT.Silu).then_inc(act_done, 1)

            def router_exp(g):
                act.wait_ge(small_done, (g - 1) * NSMALL + 2 + GB)
                nc.scalar.activation(small[:, 64:64 + GB * NE], small[:, 64:64 + GB * NE], ACT.Exp).then_inc(lexp_done, 1)

            def between(g, experts, ahead):
                j = g + 1
                if ahead:
                    transposed("a", j, xt_a, 0)
                if experts:
                    transposed("e", g - 1, xt_e, 6)
                    if not ahead:
                        experts_silu(g)
                for q in range(NQ if ahead else 0):
                    for a in range(2):
                        ic = 2 * q + a
                        if a == 0:
                            if q >= 2:
                                act.wait_ge(u_done, j * NQ + q - 1)
                            act.wait_ge(hin_ps, j * NQ + q + 1)
                        nc.scalar.activation(hc0[:, ic % 4, :], ps[:, q % 2, a * NT:(a + 1) * NT], ACT.Identity,
                                             scale=conv_w[:, ic, KC - 1:KC], bias=conv_b[:, ic:ic + 1]).then_inc(tap3_done, 1)
                    act.wait_ge(gin_ps, j * NQ + q + 1)
                    nc.scalar.activation(gate[:, 2 * q:2 * q + 2, :].rearrange("p a t -> p (a t)"), ps[:, 2 + q % 2, :],
                                         ACT.Silu).then_inc(gate_done, 1)
                    if q:
                        act.wait_ge(conv_done, j * NI + 2 * q)
                        nc.scalar.activation(u[:, 2 * q - 2:2 * q, :], hc0[:, (2 * q - 2) % 4:(2 * q - 2) % 4 + 2, :],
                                             ACT.Silu).then_inc(u_done, 1)
                    if experts and q == 0:
                        experts_silu(g)
                    if experts and q == 1:
                        router_exp(g)
                if ahead:
                    act.wait_ge(conv_done, (j + 1) * NI)
                    nc.scalar.activation(u[:, NI - 2:NI, :], hc0[:, 2:4, :], ACT.Silu).then_inc(u_done, 1)
                if experts and not ahead:
                    router_exp(g)
                if ahead:
                    act.wait_ge(ts_ps, j + 1)
                    nc.scalar.copy(ts[:], ps[:, 4, 0:NT]).then_inc(ts_done, 1)
                    for q in range(NQ):
                        for a in range(2):
                            ic = 2 * q + a
                            act.wait_ge(dt_ps, j * NQ + q + 1)
                            nc.scalar.activation(delta[:, ic, :], ps[:, 2 + q % 2, a * NT:(a + 1) * NT], ACT.Identity,
                                                 bias=dt_b[:, ic:ic + 1]).then_inc(z_done, 1)
                        if q == 1:
                            act.wait_ge(z_done, j * NI + 2)
                            soft_parts(j * NQ, 0)
                    for q in range(0, 8, 2):
                        act.wait_ge(rep_ps, j * 8 + q + 1)
                        nc.scalar.copy(bc[:, 4 * q:4 * q + 4, :].rearrange("p (k a) t -> p k (a t)", k=2),
                                       ps[:, 2 * (q % 4):2 * (q % 4) + 2, :]).then_inc(rep_a, 1)
                    act.wait_ge(z_done, (j + 1) * NI)
                    act.wait_ge(da_zeroed, j + 1)

            between(-1, False, True)
            scans(0, False)
            between(0, False, True)
            with act.Fori(1, NG - 1) as g:
                scans(g, True)
                between(g, True, True)
            scans(NG - 1, True)
            between(NG - 1, True, False)
            scans(NG, True, False)
            between(NG, True, False)

        @block.tensor
        def _(pe):
            pe.wait_ge(w_loaded, ALL_W)
            nc.tensor.matmul(ps[:, 0, 0:1], w_o[:, 0, :], b_v[:, 0:1], start=True, stop=False)
            nc.tensor.matmul(ps[:, 0, 0:1], w_o[:, 1, :], b_v[:, 1:2], start=False, stop=True).then_inc(bo_ps, 1)
            pe.wait_ge(bo_done, 1)
            pe.wait_ge(att_zero, 3)

            def transposes(use, j, xn, bank):
                pe.wait_ge(ln_out[use], (j + 1) * GB)
                for k in range(KH):
                    for b in range(GB):
                        at = (k % 2) * NT + b * T
                        last = nc.tensor.transpose(ps[:, bank + k // 2, at:at + T], xn[:, b, k * P:(k + 1) * P], ident[:])
                    if k % 2:
                        last.then_inc(xt_ps[use], 1)

            def attention_part(i, what, n=0):
                if what == "proj":
                    pe.wait_ge(xb_done, i + 1)
                    for j in range(4):
                        nc.tensor.matmul(ps[:, PS_ATT + j, :], w_qk[:, j, :], xb[:], start=True, stop=True).then_inc(qk_ps, 1)
                    pe.wait_ge(qk_done, i * 4 + 1)
                    for kb in range(NBLK):
                        last = nc.tensor.matmul(ps[:, PS_ATT, kb * P:(kb + 1) * P], xb[:, kb * P:(kb + 1) * P], w_v[:],
                                                start=True, stop=True)
                    last.then_inc(v_ps, 1)
                elif what == "s":
                    lo, hi, at = window(n)
                    if n == 0:
                        pe.wait_ge(qk_done, i * 4 + 4)
                        pe.wait_ge(v_done, i + 1)
                    else:
                        pe.wait_ge(max_done, i * 4 + n)
                    for hp in range(4):
                        out = ps[:, PS_ATT + hp, :].rearrange("p (j w) -> p j w", j=NJ)
                        nc.tensor.matmul(out[:, :, lo:hi], ident_bf[:], band[:, 0:1, lo:hi].to_broadcast([P, NJ, hi - lo]),
                                         start=True, stop=False, skip_group_check=True)
                    for j in range(NJ):
                        for hp in range(4):
                            r = 32 * hp
                            last = nc.tensor.matmul(
                                ps[:, PS_ATT + hp, j * WIN + lo:j * WIN + hi],
                                qk[r:r + 32, j, n * P:(n + 1) * P], qk[r:r + 32, 2 + j, at:at + hi - lo],
                                start=False, stop=True, skip_group_check=True)
                    last.then_inc(s_ps, 1)
                elif what == "shift":
                    pe.wait_ge(max_done, i * 4 + 4)
                    for j in range(NJ):
                        for qb in range(NBLK):
                            last = nc.tensor.matmul(ps[:, PS_ATT + j, qb * P:(qb + 1) * P], nmax[:, qb, j, :], ident[:],
                                                    start=True, stop=True)
                        last.then_inc(shift_ps, 1)
                elif what == "st":
                    j = n // 2
                    if n == 0:
                        pe.wait_ge(q_done, i * 2 + 2)
                    elif n == 2:
                        pe.wait_ge(o_done, i * 2 + 1)
                    else:
                        pe.wait_ge(p_done, i * 8 + 2 * n)
                    blks = [2 * (n % 2), 2 * (n % 2) + 1]
                    for hp in range(4):
                        for a, blk in enumerate(blks):
                            lo, hi, at = window(blk)
                            nc.tensor.matmul(ps[:, PS_ATT + hp, a * WIN + lo:a * WIN + hi], ident_bf[:], band[:, 0, lo:hi],
                                             start=(a == 0), stop=False, skip_group_check=True)
                    for a, blk in enumerate(blks):
                        lo, hi, at = window(blk)
                        for hp in range(4):
                            r = 32 * hp
                            last = nc.tensor.matmul(
                                ps[:, PS_ATT + hp, a * WIN + lo:a * WIN + hi],
                                qk[r:r + 32, 2 + j, blk * P:(blk + 1) * P], qk[r:r + 32, j, at:at + hi - lo],
                                start=False, stop=True, skip_group_check=True)
                    last.then_inc(st_ps, 1)
                elif what == "av":
                    pe.wait_ge(p_done, i * 8 + 4 * n + 4)
                    for kb in range(NBLK):
                        lo, hi, at = window(kb)
                        for hp in range(4):
                            last = nc.tensor.matmul(
                                ps[32 * hp:32 * hp + 32, PS_ATT, at:at + hi - lo],
                                v_aug[:, kb, 4 * n + hp, :], probs[:, hp, kb, lo:hi],
                                start=(kb == 0), stop=(kb == NBLK - 1), skip_group_check=True)
                    last.then_inc(o_ps, 1)
                elif what == "den":
                    for j in range(NJ):
                        pe.wait_ge(o_done, i * 2 + j + 1)
                        for qb in range(NBLK):
                            at = (j * NBLK + qb) * 4
                            last = nc.tensor.matmul(ps[:, PS_ATT + 1, at:at + 4], o_sb[:, j, qb * P:(qb + 1) * P], den_sel[:],
                                                    start=True, stop=True)
                    last.then_inc(den_ps, 1)
                elif what == "rep":
                    pe.wait_ge(rden_wide, i + 1)
                    for j in range(NJ):
                        for qb in range(NBLK):
                            at = (j * NBLK + qb) * 4
                            last = nc.tensor.matmul(ps[:, PS_ATT + 2 + j, qb * P:(qb + 1) * P],
                                                    rden_rep[:, 32 * at:32 * at + P],
                                                    ident[:], start=True, stop=True)
                        last.then_inc(rrep_ps, 1)
                elif what == "wo":
                    pe.wait_ge(on_done, i * 2 + 2)
                    for j in range(NJ):
                        last = nc.tensor.matmul(ps[:, PS_ATT + 3, :], w_o[:, j, :], o_sb[:, j, :], start=(j == 0), stop=(j == 1))
                    last.then_inc(wo_ps, 1)
                else:
                    pe.wait_ge(enc_used, i + 2)
                    nc.tensor.matmul(ps[:, PS_ATT, :], w_ct[:], xb[:], start=True, stop=True).then_inc(ct_ps, 1)

            def scans(g, att, scan=True):
                for s in range(SG):
                    if att and s % SB in PE_AT:
                        attention_part((g - 1) * GB + s // SB, *PE_AT[s % SB])
                    if not scan or (s + 1) % BATCH:
                        continue
                    ic, r = s // RS, s % RS
                    pe.wait_ge(hcd_done, (g * NI + ic) * NDC + dpc(r + 1))
                    pe.wait_ge(hcp_done, (g * NI + ic) * NPC + r + 1 - dpc(r + 1))
                    for t in range(s + 1 - BATCH, s + 1):
                        for n in range(2):
                            last = nc.tensor.matmul(ps[:, PS_Y + ic % 2, 0:NT], ident[:], ring[:, t % RING, n * NT:(n + 1) * NT],
                                                    start=(t % RS == 0 and n == 0), stop=(t % RS == RS - 1 and n == 1))
                        last.then_inc(hc_used, 1)

            def experts_down(g, mixer):
                if mixer:
                    pe.wait_ge(x1_done, (g + 1) * GB)
                pe.wait_ge(xt_done["e"], g * 2)
                for k in range(KH):
                    last = nc.tensor.matmul(ps[:, 4, 0:NT], w_down[:, k, :], xt_e[:, k, :], start=(k == 0), stop=(k == KH - 1))
                last.then_inc(down_ps, 1)
                for b in range(GB):
                    for k in range(KH):
                        last = nc.tensor.matmul(ps[:, 5, b * NE:(b + 1) * NE], xt_e[:, k, b * T:(b + 1) * T],
                                                w_router[:, k, :], start=(k == 0), stop=(k == KH - 1))
                last.then_inc(logit_ps, 1)

            def between(g, experts, ahead, mixer=True):
                j = g + 1
                if mixer:
                    pe.wait_ge(y_done, (g + 1) * NI)
                    if experts:
                        pe.wait_ge(x2_done, g * GB)
                    for b in range(GB):
                        for ic in range(NI):
                            if b == 0 and ic == NI - 1:
                                pe.wait_ge(y_done, (g + 1) * NI + 1)
                            last = nc.tensor.matmul(ps[:, 4 + b, :], gate[:, ic, b * T:(b + 1) * T], w_outp[:, ic, :],
                                                    start=(ic == 0), stop=(ic == NI - 1))
                        last.then_inc(outp_ps, 1)
                        if b == 0 and ahead:
                            transposes("a", j, xn_a, 0)
                elif ahead:
                    transposes("a", j, xn_a, 0)
                if experts:
                    transposes("e", g - 1, xn_e, 6)
                    if not ahead:
                        experts_down(g, mixer)
                for q in range(NQ if ahead else 0):
                    for half, made in ((0, hin_ps), (1, gin_ps)):
                        if q >= 2 and half == 0:
                            pe.wait_ge(conv_done, j * NI + 2 * q - 2)
                        elif q >= 2:
                            pe.wait_ge(gate_done, j * NQ + q - 1)
                        elif q == 0 and half == 0:
                            pe.wait_ge(xt_done["a"], (j + 1) * 2)
                        for a in range(2):
                            for k in range(KH):
                                col = half * I + (2 * q + a) * P
                                last = nc.tensor.matmul(ps[:, 2 * half + q % 2, a * NT:(a + 1) * NT], w_in[:, k, col:col + P],
                                                        xt_a[:, k, :], start=(k == 0), stop=(k == KH - 1))
                        last.then_inc(made, 1)
                    if experts and q == 0:
                        experts_down(g, mixer)
                if experts:
                    pe.wait_ge(grep_done, g)
                    for b in range(GB):
                        last = nc.tensor.matmul(ps[:, 6, b * T:(b + 1) * T], g_rep[:, b].rearrange("p e i -> p (e i)"),
                                                ident[:], start=True, stop=True)
                    last.then_inc(gt_ps, 1)
                for ic in range(NI if ahead else 0):
                    if ic == 0 and experts:
                        pe.wait_ge(act_done, g)
                        pe.wait_ge(small_done, (g - 1) * NSMALL + 1)
                    elif ic == 0 and mixer:
                        pe.wait_ge(x1_done, (g + 1) * GB)
                    if ic % 2 == 0:
                        pe.wait_ge(u_done, j * NQ + ic // 2 + 1)
                    last = nc.tensor.matmul(ps[:, 4, 0:NT], w_xt[:, ic, :], u[:, ic, :], start=(ic == 0), stop=(ic == NI - 1))
                if ahead:
                    last.then_inc(ts_ps, 1)
                if experts:
                    pe.wait_ge(gated_done, g)
                    for b in range(GB):
                        nc.tensor.matmul(ps[:, 6 + b, :], gated[:, b * T:(b + 1) * T], w_up[:], start=True, stop=True).then_inc(up_ps, 1)
                    if not ahead:
                        pe.wait_ge(x3_done, g * GB)
                if ahead:
                    pe.wait_ge(ts_done, j + 1)
                    for q in range(NQ):
                        if q == 2:
                            for ic in range(NI):
                                last = nc.tensor.matmul(ps[0:96, 5, 0:NT], w_xbc[:, ic, :], u[:, ic, :],
                                                        start=(ic == 0), stop=(ic == NI - 1))
                            last.then_inc(bc_ps, 1)
                        if q >= 2:
                            pe.wait_ge(z_done, j * NI + 2 * q - 2)
                        for a in range(2):
                            ic = 2 * q + a
                            last = nc.tensor.matmul(ps[:, 2 + q % 2, a * NT:(a + 1) * NT], w_dt[:, ic * P:(ic + 1) * P], ts[:],
                                                    start=True, stop=True)
                        last.then_inc(dt_ps, 1)
                    pe.wait_ge(split_done, j * 6 + 6)
                    pe.wait_ge(conv_done, (j + 1) * NI)
                    for q in range(8):
                        if q >= 4:
                            pe.wait_ge((rep_a, rep_v)[q % 2], j * 4 + q // 2 - 1)
                        elif q == 1:
                            pe.wait_ge(z_done, (j + 1) * NI)
                        elif q == 3 and experts:
                            pe.wait_ge(x3_done, g * GB)
                        for r in range(4):
                            s = 4 * q + r
                            last = nc.tensor.matmul(ps[:, 2 * (q % 4) + r // 2, (r % 2) * NT:(r % 2 + 1) * NT],
                                                    stack3[:, s:s + 1].to_broadcast([96, P]), bc_st, start=True, stop=True)
                        last.then_inc(rep_ps, 1)
                    pe.wait_ge(rep_a, j * 4 + 4)
                    pe.wait_ge(rep_v, j * 4 + 4)

            between(-1, False, True, False)
            scans(0, False)
            between(0, False, True)
            with pe.Fori(1, NG - 1) as g:
                scans(g, True)
                between(g, True, True)
            scans(NG - 1, True)
            between(NG - 1, True, False)
            scans(NG, True, False)
            between(NG, True, False, False)

        @block.vector
        def _(dve):
            dve.wait_ge(a_exp, 1)
            dve.wait_ge(const_done, 1)
            nc.vector.tensor_scalar(a_neg[:], a_neg[:], -1.0, None, ALU.mult).then_inc(setup_done, 1)
            nc.vector.tensor_scalar(b_qk[:, 0:NJ], b_qk[:, 0:NJ], 0.25, None, ALU.mult).then_inc(setup_done, 1)
            dve.sem_inc(h_done, H0)
            dve.sem_inc(hc_used, U0)
            dve.sem_inc(dt_done, 1)
            dve.sem_inc(y_done, 1)
            dve.sem_inc(enc_used, 1)
            dve.wait_ge(att_zero, 3)

            def hold():
                nc.vector.tensor_copy(held[:], neg_half[:, 0:1])

            def norm_stats(use, j, src):
                for b in range(GB):
                    nc.vector.bn_stats(ln_st[use][:, b, :], src[:, b, :]).then_inc(ln_stat[use], 1)
                dve.wait_ge(ln_stat[use], (j + 1) * GB)
                hold()
                for b in range(GB):
                    nc.vector.bn_aggr(ln_mv[use][:, b, :], ln_st[use][:, b, :]).then_inc(ln_aggr[use], 1)
                dve.wait_ge(ln_aggr[use], (j + 1) * GB)
                nc.vector.tensor_scalar(ln_rs[use][:], ln_mv[use][:, :, 1], EPS, None, ALU.add).then_inc(ln_eps[use], 1)

            def normalise(use, j, dst, src):
                dve.wait_ge(ln_rstd[use], j + 1)
                for b in range(GB):
                    nc.vector.tensor_scalar(dst[:, b, :], src[:, b, :], ln_mv[use][:, b, 0:1], ln_rs[use][:, b:b + 1],
                                            ALU.subtract, ALU.mult).then_inc(ln_out[use], 1)

            def soft_step(s, g, pq, q):
                z = delta[:, 2 * q:2 * q + 2, :].rearrange("p a t -> p (a t)")
                if s == -2:
                    dve.wait_ge(dt_done, pq + 1)
                    if q == 0:
                        dve.wait_ge(z_done, g * NI + 2)
                    nc.vector.tensor_scalar(pos[:], z, 0.0, None, ALU.max).then_inc(sp_pos, 1)
                elif s == -1:
                    dve.wait_ge(sp_exp, pq + 1)
                    nc.vector.tensor_scalar(tmp[:], soft[:], 1.0, 1.0, ALU.add, ALU.subtract).then_inc(sp_r, 1)
                elif s == 0:
                    dve.wait_ge(sp_r, pq + 1)
                    nc.vector.tensor_tensor(tmp[:], soft[:], tmp[:], ALU.subtract).then_inc(sp_c, 1)
                elif s == 1:
                    dve.wait_ge(sp_pos, pq + 1)
                    dve.wait_ge(sp_c, pq + 1)
                    nc.vector.tensor_tensor(tmp[:], tmp[:], pos[:], ALU.add).then_inc(sp_d, 1)
                elif s == 2:
                    dve.wait_ge(sp_d, pq + 1)
                    dve.wait_ge(sp_ln, pq + 1)
                    nc.vector.tensor_tensor(z, z, tmp[:], ALU.add).then_inc(dt_done, 1)
                else:
                    dve.wait_ge(dt_done, pq + 2)
                    nc.vector.tensor_tensor(du[:, q % 2, :], z, u[:, 2 * q:2 * q + 2, :].rearrange("p a t -> p (a t)"),
                                            ALU.mult).then_inc(du_done, 1)

            def times_c(g, s):
                r = s % RS
                dve.wait_ge(h_done, H0 + 1 + g * SG + s)
                nc.vector.tensor_tensor(ring[:, s % RING, :], ring[:, s % RING, :],
                                        bc[:, N + 2 * r:N + 2 * r + 2, :].rearrange("p a t -> p (a t)"),
                                        ALU.mult).then_inc(hcd_done, 1)

            def y_step(g, ic, s):
                if s == 0:
                    dve.wait_ge(hc_used, U0 + g * SG + (ic + 1) * RS)
                    dve.wait_ge(y_done, g * NI + ic + 1)
                    nc.vector.scalar_tensor_tensor(y_tmp[:], u[:, ic, :], d_skip[:, ic:ic + 1], ps[:, PS_Y + ic % 2, 0:NT],
                                                   ALU.mult, ALU.add).then_inc(y_sum, 1)
                else:
                    dve.wait_ge(y_sum, g * NI + ic + 1)
                    nc.vector.tensor_tensor(gate[:, ic, :], y_tmp[:], gate[:, ic, :], ALU.mult).then_inc(y_done, 1)

            def attention_part(g, b, what, n=0):
                i = g * GB + b
                if what == "xb":
                    if not b:
                        return
                    dve.wait_ge(ct_ps, i)
                    nc.vector.tensor_scalar(xb[:], x_att[:, b, :], ln_mv["t"][:, b, 0:1], ln_rs["t"][:, b:b + 1],
                                            ALU.subtract, ALU.mult).then_inc(xb_done, 1)
                elif what == "v":
                    dve.wait_ge(v_ps, i + 1)
                    nc.vector.tensor_copy(v_aug[:, :, :, 0:DH].rearrange("p k h d -> p (k h) d"),
                                          ps[:, PS_ATT, :].rearrange("p (a d) -> p a d", d=DH)).then_inc(v_done, 1)
                elif what == "max":
                    lo, hi, _ = window(n)
                    dve.wait_ge(s_ps, i * 4 + n + 1)
                    nc.vector.tensor_reduce(
                        nmax[:, n].rearrange("p j (a r) -> p a j r", r=32)[:, :, :, DH],
                        ps[:, PS_ATT:PS_ATT + 4, :].rearrange("p a (j w) -> p a j w", j=NJ)[:, :, :, lo:hi],
                        AX.X, ALU.max, negate=True).then_inc(max_done, 1)
                elif what == "addq":
                    for j in range(NJ):
                        dve.wait_ge(shift_ps, i * 2 + j + 1)
                        nc.vector.tensor_tensor(qk[:, j, :], ps[:, PS_ATT + j, :], qk[:, j, :], ALU.add).then_inc(q_done, 1)
                elif what == "rden":
                    dve.wait_ge(den_ps, i + 1)
                    nc.vector.reciprocal(rden[:], ps[:, PS_ATT + 1, 0:NBLK * NHEAD]).then_inc(rden_done, 1)
                elif what == "on":
                    for j in range(NJ):
                        dve.wait_ge(rrep_ps, i * 2 + j + 1)
                        nc.vector.tensor_tensor(o_sb[:, j, :], ps[:, PS_ATT + 2 + j, :], o_sb[:, j, :], ALU.mult).then_inc(on_done, 1)
                elif what == "enc":
                    dve.wait_ge(enc_in, (i + 1) * 16)
                    dve.wait_ge(relu_done, i + 1)
                    nc.vector.tensor_tensor(xb[:], xb[:], enc[:], ALU.mult).then_inc(enc_used, 1)
                else:
                    dve.wait_ge(ct_ps, i + 1)
                    nc.vector.scalar_tensor_tensor(x_att[:, b, :], ps[:, PS_ATT, :], b_ct[:], x_att[:, b, :],
                                                   ALU.add, ALU.add).then_inc(x2_done, 1)

            def scans(g, att, scan=True):
                for s in range(SG):
                    ic, r = s // RS, s % RS
                    if scan:
                        dve.wait_ge(da_done, (g * SG + s + 1) * 2)
                        dve.wait_ge(dbx_done, g * SG + s + 1)
                        nc.vector.tensor_tensor_scan(ring[:, s % RING, :], ps[:, s % DAR, :], ring[:, s % RING, :], 0.0,
                                                     ALU.mult, ALU.add).then_inc(h_done, 1)
                        if s and (s - 1) % RS not in POOL_C:
                            times_c(g, s - 1)
                        if s % (2 * RS) in SOFT_AT and ic // 2 < NQ - 1:
                            soft_step(SOFT_AT[s % (2 * RS)], g, g * NQ + ic // 2 + 1, ic // 2 + 1)
                        if ic and r in (5, 6):
                            y_step(g, ic - 1, r - 5)
                    if att and s % SB in DVE_AT:
                        attention_part(g - 1, s // SB, *DVE_AT[s % SB])
                if scan:
                    times_c(g, SG - 1)
                    y_step(g, NI - 1, 0)
                    y_step(g, NI - 1, 1)

            lg = small[:, 0:GB * NE].rearrange("p (b e) -> p b e", b=GB)
            top = small[:, 32:32 + GB * NE].rearrange("p (b e) -> p b e", b=GB)
            ex = small[:, 64:64 + GB * NE].rearrange("p (b e) -> p b e", b=GB)
            tot, rtot = small[:, 96:96 + GB], small[:, 100:100 + GB]
            idx = small[:, 128:128 + GB * NE].bitcast(U32).rearrange("p (b e) -> p b e", b=GB)
            idf = small[:, 160:160 + 2 * GB].rearrange("p (b s) -> p b s", b=GB)
            eq = small[:, 168:168 + 2 * GB * NE].rearrange("p (b s e) -> p b s e", b=GB, s=2)
            wt = small[:, 208:208 + GB * NE].rearrange("p (b e) -> p b e", b=GB)
            wt_rep = small[:, 208:208 + GB * NE].rearrange("p (b e o) -> p b e o", b=GB, o=1)

            def router(j, part):
                def after(k):
                    dve.wait_ge(small_done, j * NSMALL + k)
                if part == 0:
                    dve.wait_ge(logit_ps, j + 1)
                    nc.vector.tensor_copy(lg, ps[:, 5, 0:GB * NE].rearrange("p (b e) -> p b e", b=GB)).then_inc(small_done, 1)
                    after(1)
                    hold()
                    for b in range(GB):
                        nc.vector.max(top[:, b, :], lg[:, b, :]).then_inc(small_done, 1)
                    after(1 + GB)
                    nc.vector.tensor_tensor(ex, lg, top[:, :, 0:1].to_broadcast([P, GB, NE]), ALU.subtract).then_inc(small_done, 1)
                    return
                n = 2 + GB
                dve.wait_ge(lexp_done, j + 1)
                nc.vector.tensor_reduce(tot, ex, AX.X, ALU.add).then_inc(small_done, 1)
                after(n + 1)
                nc.vector.reciprocal(rtot, tot).then_inc(small_done, 1)
                after(n + 2)
                nc.vector.tensor_tensor(wt, ex, rtot.rearrange("p (b o) -> p b o", o=1).to_broadcast([P, GB, NE]),
                                        ALU.mult).then_inc(small_done, 1)
                after(n + 3)
                hold()
                for b in range(GB):
                    nc.vector.max(top[:, b, :], wt[:, b, :])
                nc.vector.tensor_copy(lg, wt).then_inc(small_done, 1)
                after(n + 4)
                hold()
                for b in range(GB):
                    nc.vector.max_index(idx[:, b, :], top[:, b, :], wt[:, b, :])
                nc.vector.tensor_copy(lg, wt).then_inc(small_done, 1)
                after(n + 5)
                nc.vector.tensor_copy(idf, idx[:, :, 0:2]).then_inc(small_done, 1)
                after(n + 6)
                for s in range(2):
                    last = nc.vector.tensor_tensor(
                        eq[:, :, s, :], iota[:].rearrange("p (o e) -> p o e", o=1).to_broadcast([P, GB, NE]),
                        idf[:, :, s:s + 1].to_broadcast([P, GB, NE]), ALU.is_equal)
                last.then_inc(small_done, 1)
                after(n + 7)
                nc.vector.tensor_tensor(eq[:, :, 0, :], eq[:, :, 0, :], eq[:, :, 1, :], ALU.add).then_inc(gate_step, 1)
                dve.wait_ge(gate_step, j * 2 + 1)
                nc.vector.tensor_tensor(wt, wt, eq[:, :, 0, :], ALU.mult).then_inc(gate_step, 1)
                dve.wait_ge(gate_step, j * 2 + 2)
                nc.vector.tensor_copy(g_rep, wt_rep.to_broadcast([P, GB, NE, 16])).then_inc(grep_done, 1)

            def first_xb(g):
                dve.wait_ge(ln_rstd["t"], g + 1)
                nc.vector.tensor_scalar(xb[:], x_res[:, 0, :], ln_mv["t"][:, 0, 0:1], ln_rs["t"][:, 0:1],
                                        ALU.subtract, ALU.mult).then_inc(xb_done, 1)

            def between(g, experts, ahead, mixer=True, first=False):
                j = g + 1
                if experts:
                    dve.wait_ge(x2_done, g * GB)
                    norm_stats("e", g - 1, x_att)
                if ahead:
                    dve.wait_ge(x_in, (j + 1) * 16)
                    norm_stats("a", j, x_new)
                    normalise("a", j, xn_a, x_new)
                if experts:
                    normalise("e", g - 1, xn_e, x_att)
                if mixer:
                    dve.wait_ge(xres_in, (g + 1) * 16)
                    for b in range(GB):
                        dve.wait_ge(outp_ps, g * GB + b + 1)
                        nc.vector.tensor_tensor(x_res[:, b, :], ps[:, 4 + b, :], x_res[:, b, :], ALU.add).then_inc(x1_done, 1)
                    dve.wait_ge(x1_done, (g + 1) * GB)
                    hold()
                    norm_stats("t", g, x_res)
                    if not ahead:
                        first_xb(g)
                if experts and not ahead:
                    router(g - 1, 0)
                for ic in range(NI if ahead else 0):
                    acc = hc0[:, ic % 4, :].rearrange("p (b t) -> p b t", b=GB)
                    src = ps[:, (ic // 2) % 2, (ic % 2) * NT:(ic % 2 + 1) * NT].rearrange("p (b t) -> p b t", b=GB)
                    dve.wait_ge(tap3_done, j * NI + (ic // 2) * 2 + 2)
                    for s in range(1, KC):
                        if s > 1:
                            dve.wait_ge(tap_done, (j * NI + ic) * 2 + s - 1)
                        nc.vector.scalar_tensor_tensor(acc[:, :, s:T], src[:, :, 0:T - s],
                                                       conv_w[:, ic, KC - 1 - s:KC - s], acc[:, :, s:T],
                                                       ALU.mult, ALU.add).then_inc(tap_done if s < KC - 1 else conv_done, 1)
                    if experts and ic in (1, 3):
                        router(g - 1, ic // 2)
                    if mixer and ic == 5:
                        first_xb(g)
                if experts:
                    if not ahead:
                        router(g - 1, 1)
                    dve.wait_ge(gt_ps, g)
                    dve.wait_ge(act_done, g)
                    nc.vector.tensor_tensor(gated, ps[:, 6, 0:NT], act_e, ALU.mult).then_inc(gated_done, 1)
                if ahead:
                    soft_step(-2, j, j * NQ, 0)
                if experts:
                    for b in range(GB):
                        dve.wait_ge(up_ps, (g - 1) * GB + b + 1)
                        nc.vector.tensor_tensor(x_att[:, b, :], ps[:, 6 + b, :], x_att[:, b, :], ALU.add).then_inc(x3_done, 1)
                if ahead:
                    for s in (-1, 0):
                        soft_step(s, j, j * NQ, 0)
                if ahead:
                    dve.wait_ge(bc_ps, j + 1)
                    nc.vector.tensor_copy(bc_hi, ps[0:96, 5, 0:NT]).then_inc(split_done, 1)
                    dve.wait_ge(split_done, j * 6 + 1)
                    nc.vector.tensor_tensor(bc_r1, ps[0:96, 5, 0:NT], bc_hi, ALU.subtract).then_inc(split_done, 1)
                    dve.wait_ge(split_done, j * 6 + 2)
                    nc.vector.tensor_copy(bc_mid, bc_r1).then_inc(split_done, 1)
                    nc.vector.tensor_copy(bc_st[0:32], bc_hi[0:32])
                    dve.wait_ge(split_done, j * 6 + 3)
                    nc.vector.tensor_tensor(bc_r2, bc_r1, bc_mid, ALU.subtract).then_inc(split_done, 1)
                    nc.vector.tensor_copy(bc_st[32:64], bc_mid[32:64]).then_inc(split_done, 1)
                    dve.wait_ge(split_done, j * 6 + 5)
                    nc.vector.tensor_copy(bc_st[64:96], bc_r2[64:96]).then_inc(split_done, 1)
                if ahead:
                    for s in range(1, 4):
                        soft_step(s, j, j * NQ, 0)
                    for q in range(1, 8, 2):
                        dve.wait_ge(rep_ps, j * 8 + q + 1)
                        nc.vector.tensor_copy(bc[:, 4 * q:4 * q + 4, :].rearrange("p (k a) t -> p k (a t)", k=2),
                                              ps[:, 2 * (q % 4):2 * (q % 4) + 2, :]).then_inc(rep_v, 1)
                    dve.wait_ge(rep_a, j * 4 + 4)
                    nc.vector.memset(ps[:, 0:DAR, :].rearrange("p s (n t) -> p s n t", t=T)[:, :, :, 0:1], 0.0).then_inc(da_zeroed, 1)
                if mixer:
                    dve.wait_ge(xb_done, g * GB + 1)
                    if not first:
                        dve.wait_ge(x_out, g * 16)
                    nc.vector.tensor_copy(x_att[:], x_res[:]).then_inc(x1_copied, 1)

            between(-1, False, True, False)
            scans(0, False)
            between(0, False, True, first=True)
            with dve.Fori(1, NG - 1) as g:
                scans(g, True)
                between(g, True, True)
            scans(NG - 1, True)
            between(NG - 1, True, False)
            scans(NG, True, False)
            between(NG, True, False, False)


def kernel(**inputs):
    import numpy as np
    import ml_dtypes
    import concourse.bacc as bacc
    from concourse.bass_utils import run_bass_kernel_spmd

    a = {k: np.asarray(v) for k, v in inputs.items()}
    P, DH, NHEAD, NJ = 128, 16, 8, 2

    def chunks(w):
        return np.ascontiguousarray(np.swapaxes(w.reshape(-1, P, *w.shape[1:]), 0, 1))

    def pad_heads(w):
        out = np.zeros((NJ, 4, 32) + w.shape[1:], np.float32)
        out[:, :, :DH] = w.reshape((NJ, 4, DH) + w.shape[1:])
        return out.reshape((NJ, P) + w.shape[1:])

    w_in, b_in = a["L0_xattn_w_in"], a["L0_xattn_b_in"]
    xp = a["L0_attn_x_proj_w"].T
    w_qk = np.concatenate([pad_heads(w_in[0:P]), pad_heads(w_in[P:2 * P])])
    b_qk = np.concatenate([pad_heads(b_in[0:P]), pad_heads(b_in[P:2 * P])]).T.copy()
    b_qk.reshape(4, 32, 4)[:, DH, 2:4] = 1.0
    row, col = np.arange(P)[:, None], np.arange(2 * P)[None, :]
    outside = np.abs(col - 64 - row) > 64
    band = np.zeros((P, 1, 2 * P), np.float32)
    band[:, 0][outside] = -1e37
    den = np.zeros((P, 4), np.float32)
    for hp in range(4):
        den[32 * hp + DH, hp] = 1.0
    bf = ml_dtypes.bfloat16
    f = np.ascontiguousarray
    feeds = {
        "x": a["x"], "ctx": a["ctx_2048"],
        "w_in": chunks(a["L0_attn_in_proj_w"].T),
        "conv_w": chunks(a["L0_attn_conv_w"][:, 0, :]), "conv_b": chunks(a["L0_attn_conv_b"]),
        "w_xt": chunks(xp[:, 0:P]), "w_xbc": chunks(np.tile(xp[:, P:], (1, 3))),
        "w_dt": f(a["L0_attn_dt_proj_w"].T), "dt_b": chunks(a["L0_attn_dt_proj_b"]),
        "a_log": chunks(a["L0_attn_A_log"]), "d_skip": chunks(a["L0_attn_D"]),
        "w_outp": chunks(a["L0_attn_out_proj_w"].T),
        "w_qk": f(w_qk.transpose(2, 0, 1)), "b_qk": f(b_qk),
        "w_v": f(w_in[2 * P:].T), "b_v": f(pad_heads(b_in[2 * P:]).T),
        "w_o": f(pad_heads(a["L0_xattn_w_out"].T).transpose(1, 0, 2)), "b_o": a["L0_xattn_b_out"].reshape(P, 1),
        "w_ct": a["L0_xattn_w_ct"], "b_ct": a["L0_xattn_b_ct"].reshape(P, 1),
        "w_router": chunks(a["L0_ffn_router_w"].T),
        "w_down": chunks(a["L0_ffn_down_w"].reshape(P, -1).T),
        "w_up": f(a["L0_ffn_up_w"].transpose(0, 2, 1).reshape(P, -1)),
        "ident": np.eye(P, dtype=np.float32), "ident_bf": np.eye(P).astype(bf), "band": band.astype(bf),
        "stack": np.tile(np.eye(32), (3, 1)).astype(bf), "den": den,
        "iota": np.tile(np.arange(8, dtype=np.float32), (P, 1)),
    }
    nc = bacc.Bacc("TRN2", target_bir_lowering=False, num_devices=1)
    aps = [nc.dram_tensor(f"in_{k}", v.shape, mybir.dt.from_np(v.dtype), kind="ExternalInput").ap()
           for k, v in feeds.items()]
    out = nc.dram_tensor("out", a["x"].shape, mybir.dt.float32, kind="ExternalOutput").ap()
    decoder_layer(nc, *aps, out)
    r = run_bass_kernel_spmd(nc, [{f"in_{k}": v for k, v in feeds.items()}], core_ids=[0])
    return r.results[0]["out"]
```
